# Optimizing a Trainium2 kernel written in Bass

```python
import numpy as np
import jax
import jax.numpy as jnp

def _softmax(x, axis=-1):
    return jax.nn.softmax(x, axis=axis)

def _gelu(x):
    return jax.nn.gelu(x, approximate=True)

def _silu(x):
    return jax.nn.silu(x)

def _sigmoid(x):
    return jax.nn.sigmoid(x)

def _layernorm(x, axis=-1, eps=1e-05):
    m = jnp.mean(x, axis=axis, keepdims=True)
    v = jnp.var(x, axis=axis, keepdims=True)
    return (x - m) / jnp.sqrt(v + eps)

def _scatter_add(tgt, idx, src, axis=0):
    return tgt.at[idx].add(src)

def _segment_sum(src, seg, n):
    return jax.ops.segment_sum(src, seg, n)
kernel_name = 'mk_xattn_ffn_d1_seqx_r8_8c0a59'

def setup_inputs(seed: int=0):
    np.random.seed(seed)
    _w = jnp.asarray

    def _rec_inputs():
        import jax
        import jax.numpy as jnp
        _rk = jax.random.key(seed)
        x = 2.818e-05 + 1 * jax.random.normal(jax.random.fold_in(_rk, 1), (32, 64, 128), jnp.float32)
        _lenS = 64 - jax.random.randint(jax.random.fold_in(_rk, 7), (32,), 0, max(1, 64 // 4) + 1, jnp.int32)
        _lenS2 = 64 - jax.random.randint(jax.random.fold_in(_rk, 8), (32,), 0, max(1, 64 // 4) + 1, jnp.int32)
        _ctx_1024P = jax.random.normal(jax.random.fold_in(_rk, 11), (32, 16, 128), jnp.float32)
        _ctx_1024c = jax.random.dirichlet(jax.random.fold_in(_rk, 511), 0.3 * jnp.ones((16,), jnp.float32), (32, 64))
        _ctx_1024t = jnp.einsum('bsk,bkd->bsd', _ctx_1024c, _ctx_1024P)
        _ctx_1024t = _ctx_1024t * jax.lax.rsqrt(jnp.mean(jnp.square(_ctx_1024t)) + 1e-12) * 0.953939
        ctx_1024 = -0.000392918 + 0.999932 * (_ctx_1024t + 0.3 * jax.random.normal(jax.random.fold_in(_rk, 611), (32, 64, 128), jnp.float32))
        return (x, ctx_1024)
    x, ctx_1024 = _rec_inputs()

    def _L0_xattn_setup():
        import jax, jax.numpy as jnp
        import numpy as np
        B, L, D = (8, 256, 128)
        key = jax.random.key(seed)
        k1, k2, k3 = jax.random.split(key, 3)
        enc_outputs = jax.random.normal(k1, (B, L, D), dtype=jnp.float32)
        x = jax.random.normal(k2, (B, L, D), dtype=jnp.float32)
        Wq = jax.random.normal(k3, (D, D), dtype=jnp.float32) * (1.0 / np.sqrt(D))
        return {'enc_outputs': enc_outputs, 'x': x, 'Wq': Wq}
    _L0_xattn_all = _L0_xattn_setup()
    _L0_xattn_in = {k: v for k, v in _L0_xattn_all.items() if k in ('Wq',)}
    del _L0_xattn_all

    def _L0_ffn_setup():
        import jax, jax.numpy as jnp
        import numpy as np
        TOP_K = 2
        N_EXPERTS = 8
        key = jax.random.key(seed)
        k_x, k_g, k_w1, k_w2 = jax.random.split(key, 4)
        B, S, d_in, d_hid, d_out, E = (8, 256, 128, 256, 128, N_EXPERTS)
        s_gate = float(np.sqrt(6.0 / (d_in + E)))
        s_w1 = float(np.sqrt(6.0 / (d_in + d_hid)))
        s_w2 = float(np.sqrt(6.0 / (d_hid + d_out)))
        x = jax.random.normal(k_x, (B, S, d_in), dtype=jnp.float32)
        gate_W = jax.random.uniform(k_g, (d_in, E), jnp.float32, -s_gate, s_gate)
        W1 = jax.random.uniform(k_w1, (E, d_in, d_hid), jnp.float32, -s_w1, s_w1)
        b1 = jnp.zeros((E, d_hid), jnp.float32)
        W2 = jax.random.uniform(k_w2, (E, d_hid, d_out), jnp.float32, -s_w2, s_w2)
        b2 = jnp.zeros((E, d_out), jnp.float32)
        return {'x': x, 'gate_W': gate_W, 'W1': W1, 'b1': b1, 'W2': W2, 'b2': b2}
    _L0_ffn_all = _L0_ffn_setup()
    _L0_ffn_in = {k: v for k, v in _L0_ffn_all.items() if k in ('gate_W', 'W1', 'b1', 'W2', 'b2')}
    del _L0_ffn_all
    return {'x': x, 'ctx_1024': ctx_1024, 'L0_xattn_Wq': _L0_xattn_in['Wq'], 'L0_ffn_gate_W': _L0_ffn_in['gate_W'], 'L0_ffn_W1': _L0_ffn_in['W1'], 'L0_ffn_b1': _L0_ffn_in['b1'], 'L0_ffn_W2': _L0_ffn_in['W2'], 'L0_ffn_b2': _L0_ffn_in['b2']}

def reference(x, ctx_1024, L0_xattn_Wq, L0_ffn_gate_W, L0_ffn_W1, L0_ffn_b1, L0_ffn_W2, L0_ffn_b2):
    import jax
    import jax.numpy as jnp

    def _L0_xattn_ref(enc_outputs, x, Wq):
        import jax, jax.numpy as jnp
        import numpy as np
        B, L, D = (8, 256, 128)
        d_k = x.shape[-1]
        q = jnp.einsum('bld,hd->blh', x, Wq)
        k = jnp.einsum('bld,hd->blh', enc_outputs, Wq)
        v = k
        scores = jnp.einsum('bqh,bkh->bqk', q, k) / jnp.sqrt(jnp.float32(d_k))
        Lq, Lk = (scores.shape[1], scores.shape[2])
        causal = jnp.tril(jnp.ones((Lq, Lk), dtype=bool))
        scores = jnp.where(causal, scores, -jnp.inf)
        attn = jax.nn.softmax(scores, axis=-1)
        return jnp.einsum('bqk,bkh->bqh', attn, v)

    def _L0_ffn_ref(x, gate_W, W1, b1, W2, b2):
        import jax, jax.numpy as jnp
        import numpy as np
        TOP_K = 2
        N_EXPERTS = 8
        E = W1.shape[0]
        d_in = x.shape[-1]
        d_out = W2.shape[-1]
        x_flat = x.reshape(-1, d_in)
        logits = x_flat @ gate_W
        gates = jax.nn.softmax(logits, axis=-1)
        tk_g, tk_i = jax.lax.top_k(gates, TOP_K)
        tk_g = tk_g / (jnp.sum(tk_g, axis=-1, keepdims=True) + 1e-08)
        cw = jnp.sum(jax.nn.one_hot(tk_i, E, dtype=x.dtype) * tk_g[..., None], axis=1)
        out = x_flat
        for e in range(E):
            h = jax.nn.relu(x_flat @ W1[e] + b1[e])
            out = out + cw[:, e:e + 1] * (h @ W2[e] + b2[e])
        return out.reshape(x.shape[:-1] + (d_out,))
    x = x + _L0_xattn_ref(ctx_1024, _layernorm(x, axis=-1), L0_xattn_Wq)
    x = x + _L0_ffn_ref(_layernorm(x, axis=-1), L0_ffn_gate_W, L0_ffn_W1, L0_ffn_b1, L0_ffn_W2, L0_ffn_b2)
    return x

_drawn_inputs = setup_inputs


def setup_inputs(seed=0):
    import zlib

    import numpy as np

    out = dict(_drawn_inputs(seed))
    spreads = {'L0_ffn_b1': (0.0, 0.296), 'L0_ffn_b2': (0.0, 0.1)}
    factors = {}
    for name, (base, spread) in spreads.items():
        noise = np.random.default_rng([zlib.crc32(name.encode()), seed]).standard_normal(out[name].shape)
        drawn = base * np.exp(spread * noise) if base else spread * noise
        out[name] = jnp.asarray(drawn.astype(out[name].dtype))
    for name, factor in factors.items():
        out[name] = (out[name] * factor).astype(out[name].dtype)
    return out
```

```python
import concourse.bass as bass
from concourse import mybir
from contextlib import ExitStack

fp32 = mybir.dt.float32
fp16 = mybir.dt.float16
i32 = mybir.dt.int32
ALU = mybir.AluOpType
ACT = mybir.ActivationFunctionType
AX = mybir.AxisListType


class Chain:

    def __init__(self, engine, semaphore, base=0):
        self.engine, self.semaphore, self.base, self.count = engine, semaphore, base, 0

    def mark(self, instruction):
        instruction.then_inc(self.semaphore, 1)
        self.count += 1

    def wait(self):
        self.engine.wait_ge(self.semaphore, self.base + self.count)

    def link(self, instruction):
        self.mark(instruction)
        self.wait()


def xattn_moe(nc, x, ctx, wq, gate_w, w1, b1, w2, b2, out):
    P = 128
    BATCH, SEQ, D = x.shape
    E, _, HID = w1.shape
    TOKENS = BATCH * SEQ
    TILES = TOKENS // P
    TG = 4
    GROUPS = TILES // TG
    GT = TG * P
    C = HID // P
    EPS = 1e-5
    SCALE = float(D) ** -0.5
    MASKED = 1e30
    SX, SW, SH = 16.0, 64.0, 16.0
    HB = 4
    LO_CREDIT, Y_CREDIT, YF_CREDIT = HB, 1, 2
    NB2 = 3 * 32

    x_v = x.rearrange("b s d -> (b s) d").rearrange("(t p) d -> p t d", p=P)
    ctx_v = ctx.rearrange("b s d -> (b s) d").rearrange("(t p) d -> p t d", p=P)
    out_v = out.rearrange("b s d -> (b s) d").rearrange("(t p) d -> p t d", p=P)
    w2_v = w2.rearrange("e (c p) n -> e p c n", p=P)

    stack = ExitStack()
    with stack:
        def sb(name, shape, dt=fp32):
            return stack.enter_context(nc.sbuf_tensor(name, shape, dt))

        def bank(name):
            return stack.enter_context(nc.psum_tensor(name, [P, 512], fp32))

        def sem(name):
            return stack.enter_context(nc.semaphore(name))

        x_sb = sb("x_sb", [P, TILES, D])
        ctx_sb = sb("ctx_sb", [P, TG, D])
        wq_sb = sb("wq_sb", [P, D])
        gate_sb = sb("gate_sb", [P, E])
        b1_rows = sb("b1_rows", [E * C, P])
        b2_rows = sb("b2_rows", [NB2, D])
        w1_sb = sb("w1_sb", [P, E, HID])
        w2_sb = sb("w2_sb", [P, E, C, D])
        ident = sb("ident", [P, P])
        ident16 = sb("ident16", [P, P], fp16)
        mask = sb("mask", [P, P])
        restart = sb("restart", [P, TG, E])
        half = sb("half", [P, TILES])
        gram = sb("gram", [P, D])
        wqT = sb("wqT", [P, D])
        b1T = sb("b1T", [P, E * C])
        w1_hi = sb("w1_hi", [P, E, HID], fp16)
        w1_lo = sb("w1_lo", [P, E, HID], fp16)
        w2_hi = sb("w2_hi", [P, E, C, D], fp16)
        w2_lo = sb("w2_lo", [P, E, C, D], fp16)
        gate_hi = sb("gate_hi", [P, E], fp16)
        gate_lo = sb("gate_lo", [P, E], fp16)
        b2_cat = sb("b2_cat", [NB2, D], fp16)
        stats = sb("stats", [P, TILES, 6])
        mv = sb("mv", [P, TILES, 2])
        rstd = sb("rstd", [P, TILES])
        xn = sb("xn", [P, TG, D])
        xnT = sb("xnT", [P, TG, P])
        ctxT = sb("ctxT", [P, TG, P])
        gT = sb("gT", [P, TG, P])
        neg_s = sb("neg_s", [P, TG, P])
        neg_max = sb("neg_max", [P, TG])
        probs = sb("probs", [P, TG, P])
        row_sum = sb("row_sum", [P, TG])
        inv_sum = sb("inv_sum", [P, TG])
        probsT = sb("probsT", [P, TG, P])
        uT = sb("uT", [P, TG, P])
        x1 = sb("x1", [P, TG, D])
        stats2 = sb("stats2", [P, TG, 6])
        mv2 = sb("mv2", [P, TG, 2])
        var2 = sb("var2", [P, TG])
        rstd2 = sb("rstd2", [P, TG])
        xf = sb("xf", [P, TG, D])
        logits = sb("logits", [P, TG, E])
        top8 = sb("top8", [P, TG, 8])
        below = sb("below", [P, TG, E])
        gate_exp = sb("gate_exp", [P, TG, E])
        is_second = sb("is_second", [P, TG, E])
        nth = sb("nth", [P, TG, E])
        one_above = sb("one_above", [P, TG])
        above = sb("above", [P, TG, E])
        chosen = sb("chosen", [P, TG, E])
        sum_two = sb("sum_two", [P, TG])
        sum_all = sb("sum_all", [P, TG])
        inv_two = sb("inv_two", [P, TG])
        weight = sb("weight", [P, TG, E])
        weight_y = sb("weight_y", [P, TG, E])
        weight_cat = sb("weight_cat", [P, TG, NB2], fp16)
        weight_catT = sb("weight_catT", [NB2, TG, P], fp16)
        x_hi = sb("x_hi", [P, GROUPS, GT], fp16)
        x_lo = sb("x_lo", [P, GROUPS, GT], fp16)
        h = sb("h", [P, HB, GT])
        h_hi = sb("h_hi", [P, HB, GT], fp16)
        h_lo = sb("h_lo", [P, HB, GT], fp16)
        acc = sb("acc", [P, TILES, D])

        psA, psB, psC, psD = (bank(f"ps{c}") for c in "ABCD")
        psH = [bank(f"psH{i}") for i in range(2)]
        psY = [bank(f"psY{i}") for i in range(2)]

        wq_in, small_in = sem("wq_in"), sem("small_in")
        x_in, ctx_in = [sem("x_in0"), sem("x_in_rest")], sem("ctx_in")
        w_in = [sem(f"w_in{e}") for e in range(E)]
        out_done = sem("out_done")
        const_zero, const_ready = sem("const_zero"), sem("const_ready")
        prep_ps, gram_ready, wqT_ready = sem("prep_ps"), sem("gram_ready"), sem("wqT_ready")
        b1_ready, small_hi, small_lo = sem("b1_ready"), sem("small_hi"), sem("small_lo")
        whi_ready, wlo_ready = sem("whi_ready"), sem("wlo_ready")
        var_ready, rstd_ready, xn_ready = sem("var_ready"), sem("rstd_ready"), sem("xn_ready")
        xnT_ps, xnT_ready, ctxT_ps, ctxT_ready = sem("xnT_ps"), sem("xnT_ready"), sem("ctxT_ps"), sem("ctxT_ready")
        gT_ps, gT_ready, scores_ps, neg_ready = sem("gT_ps"), sem("gT_ready"), sem("scores_ps"), sem("neg_ready")
        probs_ready, probsT_ps, probsT_ready = sem("probs_ready"), sem("probsT_ps"), sem("probsT_ready")
        uT_ps, uT_ready, attn_ps = sem("uT_ps"), sem("uT_ready"), sem("attn_ps")
        x1_ready, var2_ready, rstd2_ready = sem("x1_ready"), sem("var2_ready"), sem("rstd2_ready")
        xf_ready, xfT_ps, xhi_ready, xlo_ready = sem("xf_ready"), sem("xfT_ps"), sem("xhi_ready"), sem("xlo_ready")
        base_ready = sem("base_ready")
        logits_ps, below_ready, gate_exp_ready = sem("logits_ps"), sem("below_ready"), sem("gate_exp_ready")
        cat_ready, catT_ps, catT_ready, b2_ps, b2_added = (
            sem("cat_ready"), sem("catT_ps"), sem("catT_ready"), sem("b2_ps"), sem("b2_added"))
        z_ps, h_ready, hhi_ready, hlo_ready = sem("z_ps"), sem("h_ready"), sem("hhi_ready"), sem("hlo_ready")
        y_ps, y_used = sem("y_ps"), sem("y_used")
        dve_chain = sem("dve_chain")

        block = stack.enter_context(nc.Block())

        def tiles(t):
            return t[:, :].rearrange("p (t n) -> p t n", n=P)

        def over(ap, n):
            return ap.unsqueeze(2).broadcast_to([P, TG, n])

        @block.sync
        def _(sp):
            sp.dma_start(wq_sb[:, :], wq).then_inc(wq_in, 16)
            sp.dma_start(x_sb[:, 0:TG, :], x_v[:, 0:TG, :]).then_inc(x_in[0], 16)
            sp.dma_start(ctx_sb[:, :, :], ctx_v[:, 0:TG, :]).then_inc(ctx_in, 16)
            sp.dma_start(gate_sb[:, :], gate_w).then_inc(small_in, 16)
            sp.dma_start(b1_rows[:, :], b1.rearrange("e (c p) -> (e c) p", p=P)).then_inc(small_in, 16)
            for q in range(3):
                sp.dma_start(b2_rows[32 * q:32 * q + E, :], b2).then_inc(small_in, 16)

            def weights(e):
                sp.dma_start(w1_sb[:, e, :], w1[e, :, :]).then_inc(w_in[e], 16)
                sp.dma_start(w2_sb[:, e, :, :], w2_v[e, :, :, :]).then_inc(w_in[e], 16)

            for e in range(0, 4):
                weights(e)
            sp.dma_start(x_sb[:, TG:, :], x_v[:, TG:, :]).then_inc(x_in[1], 16)
            for e in range(4, E):
                weights(e)

            def next_context(a):
                sp.wait_ge(uT_ps, a)
                sp.dma_start(ctx_sb[:, :, :], ctx_v[:, bass.ts(a, TG), :]).then_inc(ctx_in, 16)

            def store(g):
                sp.wait_ge(y_used, YF_CREDIT + (g + 1) * E)
                sp.dma_start(out_v[:, bass.ts(g, TG), :], acc[:, bass.ts(g, TG), :]).then_inc(out_done, 16)

            next_context(1)
            for g in range(0, GROUPS - 2):
                next_context(g + 2)
                store(g)
            store(GROUPS - 2)
            store(GROUPS - 1)
            sp.wait_ge(out_done, 16 * GROUPS)

        @block.tensor
        def _(pe):
            def transposes(bank_ap, src, ready):
                for t in range(TG):
                    last = nc.tensor.transpose(bank_ap[:, t, :], src[:, t, :], ident[:, :])
                last.then_inc(ready, 1)

            def xn_ctx_transposes(a, first=False):
                pe.wait_ge(xn_ready, a + 1)
                transposes(tiles(psA), xn, xnT_ps)
                pe.wait_ge(ctx_in, 16 * (a + 1))
                if not first:
                    pe.wait_ge(below_ready, a)
                transposes(tiles(psB), ctx_sb, ctxT_ps)

            def gram_product(a):
                pe.wait_ge(xnT_ready, a + 1)
                nc.tensor.matmul(psC[:, :], gram[:, :], xnT[:, :, :], start=True, stop=True).then_inc(gT_ps, 1)

            def score_product(a):
                pe.wait_ge(gT_ready, a + 1)
                pe.wait_ge(ctxT_ready, a + 1)
                for t in range(TG):
                    last = nc.tensor.matmul(tiles(psA)[:, t, :], gT[:, t, :], ctxT[:, t, :], start=True, stop=True)
                last.then_inc(scores_ps, 1)

            def probs_transposes(a):
                pe.wait_ge(probs_ready, a + 1)
                transposes(tiles(psB), probs, probsT_ps)

            def context_product(a):
                pe.wait_ge(probsT_ready, a + 1)
                for t in range(TG):
                    last = nc.tensor.matmul(tiles(psC)[:, t, :], ctx_sb[:, t, :], probsT[:, t, :],
                                            start=True, stop=True)
                last.then_inc(uT_ps, 1)

            def value_product(a, first):
                pe.wait_ge(uT_ready, a + 1)
                if not first:
                    pe.wait_ge(b2_added, a)
                for t in range(TG):
                    last = nc.tensor.matmul(tiles(psD)[:, t, :], uT[:, t, :], wqT[:, :], start=True, stop=True)
                last.then_inc(attn_ps, 1)

            def xf_transposes(a):
                pe.wait_ge(xf_ready, a + 1)
                transposes(tiles(psA), xf, xfT_ps)

            def logit_product(a):
                pe.wait_ge(xlo_ready, a + 1)
                for t in range(TG):
                    o = psB[:, t * E:(t + 1) * E]
                    hi, lo = (v[:, a, t * P:(t + 1) * P] for v in (x_hi, x_lo))
                    nc.tensor.matmul(o, hi, gate_hi[:, :], start=True, stop=False)
                    nc.tensor.matmul(o, hi, gate_lo[:, :], start=False, stop=False)
                    last = nc.tensor.matmul(o, lo, gate_hi[:, :], start=False, stop=True)
                last.then_inc(logits_ps, 1)

            cat_ps = psD[0:NB2, 0:TG * P // 2].bitcast(fp16).rearrange("p (t n) -> p t n", n=P)

            def cat_transposes(g):
                pe.wait_ge(cat_ready, g + 1)
                for t in range(TG):
                    last = nc.tensor.transpose(cat_ps[:, t, :], weight_cat[:, t, :], ident16[:, :])
                last.then_inc(catT_ps, 1)

            def b2_product(g):
                pe.wait_ge(catT_ready, g + 1)
                for t in range(TG):
                    last = nc.tensor.matmul(tiles(psD)[:, t, :], weight_catT[:, t, :], b2_cat[:, :],
                                            start=True, stop=True)
                last.then_inc(b2_ps, 1)

            def hidden_product(g, e, first=False):
                u = (g * E + e) * C
                if e == 0:
                    pe.wait_ge(xlo_ready, g + 1)
                for c in range(C):
                    if not first:
                        pe.wait_ge(h_ready, u + c - 1)
                    w = slice(c * P, (c + 1) * P)
                    nc.tensor.matmul(psH[c][:, :], w1_hi[:, e, w], x_hi[:, g, :], start=True, stop=False)
                    nc.tensor.matmul(psH[c][:, :], w1_hi[:, e, w], x_lo[:, g, :], start=False, stop=False)
                    nc.tensor.matmul(psH[c][:, :], w1_lo[:, e, w], x_hi[:, g, :], start=False,
                                     stop=True).then_inc(z_ps, 1)

            def output_product(g, e):
                n = g * E + e
                i = e % 2
                pe.wait_ge(hlo_ready, LO_CREDIT + (n + 1) * C)
                pe.wait_ge(y_used, n + 1)
                for t in range(TG):
                    for c in range(C):
                        hi = h_hi[:, C * i + c, t * P:(t + 1) * P]
                        lo = h_lo[:, C * i + c, t * P:(t + 1) * P]
                        o = tiles(psY[i])[:, t, :]
                        nc.tensor.matmul(o, hi, w2_hi[:, e, c, :], start=(c == 0), stop=False)
                        nc.tensor.matmul(o, hi, w2_lo[:, e, c, :], start=False, stop=False)
                        last = nc.tensor.matmul(o, lo, w2_hi[:, e, c, :], start=False, stop=(c == C - 1))
                last.then_inc(y_ps, 1)

            def group(g, attention):
                a = g + 1
                slots = {3: lambda: cat_transposes(g), 5: lambda: b2_product(g)}
                if attention:
                    slots.update({1: lambda: xn_ctx_transposes(a), 2: lambda: gram_product(a),
                                  4: lambda: score_product(a), 6: lambda: probs_transposes(a),
                                  7: lambda: context_product(a), 9: lambda: value_product(a, False),
                                  12: lambda: xf_transposes(a), 14: lambda: logit_product(a)})
                for e in range(E):
                    if e < E - 1:
                        hidden_product(g, e + 1)
                    elif attention:
                        hidden_product(g + 1, 0)
                    slots.get(2 * e, lambda: None)()
                    output_product(g, e)
                    slots.get(2 * e + 1, lambda: None)()

            pe.sem_inc(y_ps, Y_CREDIT)
            pe.wait_ge(const_ready, 1)
            pe.wait_ge(wq_in, 16)
            nc.tensor.matmul(psC[:, 0:D], wq_sb[:, :], wq_sb[:, :], start=True, stop=True)
            nc.tensor.transpose(psC[:, D:2 * D], wq_sb[:, :], ident[:, :]).then_inc(prep_ps, 1)
            xn_ctx_transposes(0, first=True)
            pe.wait_ge(wqT_ready, 1)
            gram_product(0)
            pe.wait_ge(small_in, 16 * 5)
            nc.tensor.transpose(psD[:, 0:E * C], b1_rows[:, :], ident[0:E * C, 0:E * C]).then_inc(prep_ps, 1)
            score_product(0)
            probs_transposes(0)
            context_product(0)
            pe.wait_ge(b1_ready, 1)
            value_product(0, True)
            xf_transposes(0)
            pe.wait_ge(small_lo, 1)
            pe.wait_ge(wlo_ready, 1)
            hidden_product(0, 0, first=True)
            logit_product(0)
            pe.wait_ge(wlo_ready, E)
            for g in range(0, GROUPS - 1):
                group(g, True)
            group(GROUPS - 1, False)

        @block.scalar
        def _(act):
            def copy(dst, src, ready, scale=1.0):
                nc.scalar.activation(dst, src, ACT.Copy, scale=scale).then_inc(ready, 1)

            def transposed(a):
                act.wait_ge(xnT_ps, a + 1)
                copy(xnT[:, :, :], tiles(psA), xnT_ready)
                act.wait_ge(ctxT_ps, a + 1)
                copy(ctxT[:, :, :], tiles(psB), ctxT_ready)

            def gram_out(a):
                act.wait_ge(gT_ps, a + 1)
                copy(gT[:, :, :], tiles(psC), gT_ready)

            def softmax(a):
                act.wait_ge(neg_ready, a + 1)
                for t in range(TG):
                    last = nc.scalar.activation(probs[:, t, :], neg_s[:, t, :], ACT.Exp, bias=neg_max[:, t:t + 1],
                                                scale=-1.0, accum_out=row_sum[:, t:t + 1])
                last.then_inc(probs_ready, 1)

            def probs_out(a):
                act.wait_ge(probsT_ps, a + 1)
                copy(probsT[:, :, :], tiles(psB), probsT_ready)

            def context_out(a):
                act.wait_ge(uT_ps, a + 1)
                copy(uT[:, :, :], tiles(psC), uT_ready)

            def x_hi_part(a):
                act.wait_ge(xfT_ps, a + 1)
                copy(x_hi[:, a, :], psA[:, :], xhi_ready, scale=SX)

            def gate_exps(a):
                act.wait_ge(below_ready, a + 1)
                nc.scalar.activation(gate_exp[:, :, :], below[:, :, :], ACT.Exp).then_inc(gate_exp_ready, 1)

            cat_ps = psD[0:NB2, 0:TG * P // 2].bitcast(fp16).rearrange("p (t n) -> p t n", n=P)

            def cat_out(g):
                act.wait_ge(catT_ps, g + 1)
                copy(weight_catT[:, :, :], cat_ps, catT_ready)

            def hidden_relu(g, e):
                u = (g * E + e) * C
                i = e % 2
                for c in range(C):
                    act.wait_ge(z_ps, u + c + 1)
                    act.wait_ge(hlo_ready, u + c + 1)
                    nc.scalar.activation(h[:, C * i + c, :], psH[c][:, :], ACT.Relu,
                                         bias=b1T[:, e * C + c:e * C + c + 1],
                                         scale=SH / (SX * SW)).then_inc(h_ready, 1)

            def group(g, attention):
                a = g + 1
                slots = {0: lambda: gate_exps(g), 3: lambda: cat_out(g)}
                if attention:
                    slots.update({1: lambda: transposed(a), 2: lambda: gram_out(a), 5: lambda: softmax(a),
                                  6: lambda: probs_out(a), 7: lambda: context_out(a), 12: lambda: x_hi_part(a)})
                for e in range(E):
                    if e < E - 1:
                        hidden_relu(g, e + 1)
                    elif attention:
                        hidden_relu(g + 1, 0)
                    slots.get(2 * e, lambda: None)()
                    slots.get(2 * e + 1, lambda: None)()

            act.wait_ge(prep_ps, 1)
            copy(gram[:, :], psC[:, 0:D], gram_ready, scale=-SCALE)
            copy(wqT[:, :], psC[:, D:2 * D], wqT_ready)
            transposed(0)
            gram_out(0)
            act.wait_ge(prep_ps, 2)
            copy(b1T[:, :], psD[:, 0:E * C], b1_ready, scale=SH)
            act.wait_ge(b1_ready, 1)

            def weight_hi(e):
                act.wait_ge(w_in[e], 32)
                nc.scalar.activation(w1_hi[:, e, :], w1_sb[:, e, :], ACT.Copy, scale=SW)
                copy(w2_hi[:, e, :, :], w2_sb[:, e, :, :], whi_ready, scale=SW)

            weight_hi(0)
            softmax(0)
            weight_hi(1)
            probs_out(0)
            weight_hi(2)
            context_out(0)
            for e in range(3, E):
                weight_hi(e)
            x_hi_part(0)
            hidden_relu(0, 0)
            for g in range(0, GROUPS - 1):
                group(g, True)
            group(GROUPS - 1, False)

        @block.gpsimd
        def _(pool):
            nc.gpsimd.memset(ident[:, :], 0.0).then_inc(const_zero, 1)
            nc.gpsimd.memset(ident16[:, :], 0.0).then_inc(const_zero, 1)
            nc.gpsimd.memset(mask[:, :], 0.0).then_inc(const_zero, 1)
            pool.wait_ge(const_zero, 3)
            nc.gpsimd.affine_select(out=ident[:, :], in_=ident[:, :], compare_op=ALU.not_equal, fill=1.0, base=0,
                                    pattern=[[-1, P]], channel_multiplier=1).then_inc(const_ready, 1)
            nc.gpsimd.affine_select(out=ident16[:, :], in_=ident16[:, :], compare_op=ALU.not_equal, fill=1.0,
                                    base=0, pattern=[[-1, P]], channel_multiplier=1).then_inc(const_zero, 1)
            nc.gpsimd.affine_select(out=mask[:, :], in_=mask[:, :], compare_op=ALU.is_ge, fill=MASKED, base=0,
                                    pattern=[[-1, P]], channel_multiplier=1).then_inc(const_zero, 1)
            pool.wait_ge(const_zero, 5)
            nc.gpsimd.memset(mask[SEQ:P, 0:SEQ], MASKED).then_inc(const_zero, 1)
            pool.wait_ge(const_zero, 6)
            nc.gpsimd.memset(restart[:, :, :], 1.0).then_inc(const_zero, 1)
            pool.wait_ge(const_zero, 7)
            nc.gpsimd.memset(restart[:, :, 0:1], 0.0)
            nc.gpsimd.memset(half[:, :], -0.5).then_inc(const_ready, 1)
            nc.gpsimd.memset(weight_cat[:, :, :], 0.0).then_inc(const_ready, 1)
            nc.gpsimd.memset(b2_cat[:, :], 0.0).then_inc(const_ready, 1)
            pool.wait_ge(const_ready, 4)

            def inv_std(dst, var, n, ready):
                nc.gpsimd.tensor_tensor(dst, var, half[:, 0:n], ALU.pow).then_inc(ready, 1)

            def attention_rstd(a):
                pool.wait_ge(var2_ready, a + 1)
                inv_std(rstd2[:, :], var2[:, :], TG, rstd2_ready)

            def base_sum(a):
                pool.wait_ge(xf_ready, a + 1)
                nc.gpsimd.tensor_tensor(acc[:, bass.ts(a, TG), :], x1[:, :, :], xf[:, :, :],
                                        ALU.add).then_inc(base_ready, 1)

            def hidden_hi(g, e):
                n = g * E + e
                i = e % 2
                for c in range(C):
                    pool.wait_ge(h_ready, n * C + c + 1)
                    if c == 0:
                        pool.wait_ge(y_ps, n)
                    nc.gpsimd.tensor_copy(h_hi[:, C * i + c, :], h[:, C * i + c, :]).then_inc(hhi_ready, 1)

            def group(g, attention):
                for e in range(E):
                    if e < E - 1:
                        hidden_hi(g, e + 1)
                    elif attention:
                        hidden_hi(g + 1, 0)
                    if e == 5 and attention:
                        attention_rstd(g + 1)
                        base_sum(g + 1)

            pool.wait_ge(var_ready, 1)
            inv_std(rstd[:, 0:TG], mv[:, 0:TG, 1], TG, rstd_ready)
            attention_rstd(0)
            base_sum(0)
            pool.wait_ge(var_ready, 2)
            inv_std(rstd[:, TG:], mv[:, TG:, 1], TILES - TG, rstd_ready)
            nc.gpsimd.wait_ge(h_ready, 1)
            nc.gpsimd.tensor_copy(h_hi[:, 0, :], h[:, 0, :]).then_inc(hhi_ready, 1)
            nc.gpsimd.wait_ge(h_ready, 2)
            nc.gpsimd.tensor_copy(h_hi[:, 1, :], h[:, 1, :]).then_inc(hhi_ready, 1)
            for g in range(0, GROUPS - 1):
                group(g, True)
            group(GROUPS - 1, False)

        @block.vector
        def _(dve):
            def first_norm_stats(t0, t1, chain):
                for t in range(t0, t1):
                    last = nc.vector.bn_stats(stats[:, t, :], x_sb[:, t, :])
                chain.link(last)
                for t in range(t0, t1):
                    last = nc.vector.bn_aggr(mv[:, t, :], stats[:, t, :])
                chain.link(last)
                nc.vector.tensor_scalar(mv[:, t0:t1, 1], mv[:, t0:t1, 1], EPS, None, ALU.add).then_inc(var_ready, 1)

            def first_norm(g):
                for t in range(TG):
                    i = g * TG + t
                    last = nc.vector.tensor_scalar(xn[:, t, :], x_sb[:, i, :], mv[:, i, 0:1], rstd[:, bass.ds(i, 1)],
                                                   ALU.subtract, ALU.mult)
                last.then_inc(xn_ready, 1)

            def mask_and_max(a, chain):
                dve.wait_ge(scores_ps, a + 1)
                for t in range(TG):
                    last = nc.vector.tensor_tensor_reduce(
                        out=neg_s[:, t, :], in0=tiles(psA)[:, t, :], in1=mask[:, :], scale=1.0, scalar=3e38,
                        op0=ALU.add, op1=ALU.min, accum_out=neg_max[:, t:t + 1])
                last.then_inc(neg_ready, 1)

            def residual_and_norm(a, chain):
                dve.wait_ge(probs_ready, a + 1)
                chain.link(nc.vector.reciprocal(inv_sum[:, :], row_sum[:, :]))
                dve.wait_ge(attn_ps, a + 1)
                for t in range(TG):
                    last = nc.vector.scalar_tensor_tensor(
                        out=x1[:, t, :], in0=tiles(psD)[:, t, :], scalar=inv_sum[:, t:t + 1],
                        in1=x_sb[:, a * TG + t, :], op0=ALU.mult, op1=ALU.add)
                chain.link(last)
                for t in range(TG):
                    last = nc.vector.bn_stats(stats2[:, t, :], x1[:, t, :])
                chain.link(last)
                for t in range(TG):
                    last = nc.vector.bn_aggr(mv2[:, t, :], stats2[:, t, :])
                chain.link(last)
                nc.vector.tensor_scalar(var2[:, :], mv2[:, :, 1], EPS, None, ALU.add).then_inc(var2_ready, 1)

            def second_norm(a):
                dve.wait_ge(rstd2_ready, a + 1)
                for t in range(TG):
                    last = nc.vector.tensor_scalar(xf[:, t, :], x1[:, t, :], mv2[:, t, 0:1], rstd2[:, t:t + 1],
                                                   ALU.subtract, ALU.mult)
                last.then_inc(xf_ready, 1)

            def x_lo_part(a):
                dve.wait_ge(xhi_ready, a + 1)
                nc.vector.scalar_tensor_tensor(out=x_lo[:, a, :], in0=psA[:, :], scalar=SX, in1=x_hi[:, a, :],
                                               op0=ALU.mult, op1=ALU.subtract).then_inc(xlo_ready, 1)

            def gate(a, chain):
                TT = nc.vector.tensor_tensor
                dve.wait_ge(logits_ps, a + 1)
                chain.link(nc.vector.tensor_scalar(logits[:, :, :], psB[:, 0:TG * E].rearrange("p (t e) -> p t e", e=E),
                                                   1.0 / (SX * SW), None, ALU.mult))
                for t in range(TG):
                    last = nc.vector.max(top8[:, t, :], logits[:, t, :])
                chain.link(last)
                first, second = top8[:, :, 0], top8[:, :, 1]
                TT(below[:, :, :], logits[:, :, :], over(first, E), ALU.subtract).then_inc(below_ready, 1)
                TT(is_second[:, :, :], logits[:, :, :], over(second, E), ALU.is_equal)
                TT(one_above[:, :], first, second, ALU.is_gt)
                chain.link(TT(above[:, :, :], logits[:, :, :], over(second, E), ALU.is_gt))
                chain.link(nc.vector.tensor_tensor_scan(
                    nth[:, :, :].rearrange("p t e -> p (t e)"), restart[:, :, :].rearrange("p t e -> p (t e)"),
                    is_second[:, :, :].rearrange("p t e -> p (t e)"), 0.0, ALU.mult, ALU.add))
                chain.link(TT(nth[:, :, :], nth[:, :, :], over(one_above[:, :], E), ALU.add))
                chain.link(nc.vector.scalar_tensor_tensor(out=chosen[:, :, :], in0=nth[:, :, :], scalar=2.0,
                                                          in1=is_second[:, :, :], op0=ALU.is_le, op1=ALU.mult))
                chain.link(TT(chosen[:, :, :], chosen[:, :, :], above[:, :, :], ALU.add))
                dve.wait_ge(gate_exp_ready, a + 1)
                chain.link(TT(chosen[:, :, :], chosen[:, :, :], gate_exp[:, :, :], ALU.mult))
                nc.vector.reduce_sum(sum_two[:, :], chosen[:, :, :], axis=AX.X)
                chain.link(nc.vector.reduce_sum(sum_all[:, :], gate_exp[:, :, :], axis=AX.X))
                chain.link(nc.vector.scalar_tensor_tensor(out=sum_two[:, :], in0=sum_all[:, :], scalar=1e-8,
                                                          in1=sum_two[:, :], op0=ALU.mult, op1=ALU.add))
                chain.link(nc.vector.reciprocal(inv_two[:, :], sum_two[:, :]))
                chain.link(TT(weight[:, :, :], chosen[:, :, :], over(inv_two[:, :], E), ALU.mult))
                dve.wait_ge(y_used, YF_CREDIT + a * E)
                nc.vector.tensor_scalar(weight_y[:, :, :], weight[:, :, :], 1.0 / (SH * SW), None, ALU.mult)
                nc.vector.tensor_scalar(weight_cat[:, :, 64:64 + E], weight[:, :, :], SX, None, ALU.mult)
                chain.link(nc.vector.tensor_scalar(weight_cat[:, :, 0:E], weight[:, :, :], SX, None, ALU.mult))
                nc.vector.scalar_tensor_tensor(out=weight_cat[:, :, 32:32 + E], in0=weight[:, :, :], scalar=SX,
                                               in1=weight_cat[:, :, 0:E], op0=ALU.mult,
                                               op1=ALU.subtract).then_inc(cat_ready, 1)
                dve.wait_ge(cat_ready, a + 1)

            def hidden_lo(g, e):
                n = g * E + e
                i = e % 2
                for c in range(C):
                    dve.wait_ge(hhi_ready, n * C + c + 1)
                    nc.vector.tensor_tensor(h_lo[:, C * i + c, :], h[:, C * i + c, :], h_hi[:, C * i + c, :],
                                            ALU.subtract).then_inc(hlo_ready, 1)

            def add_expert(g, e, last_expert=False):
                n = g * E + e
                dve.wait_ge(y_ps, Y_CREDIT + n + 1)
                if e == 0:
                    dve.wait_ge(base_ready, g + 1)
                else:
                    dve.wait_ge(y_used, YF_CREDIT + n)
                for t in range(TG):
                    o = acc[:, g * TG + t, :]
                    last = nc.vector.scalar_tensor_tensor(out=o, in0=tiles(psY[e % 2])[:, t, :],
                                                          scalar=weight_y[:, t, e:e + 1], in1=o,
                                                          op0=ALU.mult, op1=ALU.add)
                last.then_inc(y_used, 1)

            def add_b2(g):
                dve.wait_ge(b2_ps, g + 1)
                dve.wait_ge(y_used, YF_CREDIT + g * E + 3)
                o = acc[:, bass.ts(g, TG), :]
                nc.vector.scalar_tensor_tensor(out=o, in0=tiles(psD), scalar=1.0 / (SX * SW), in1=o,
                                               op0=ALU.mult, op1=ALU.add).then_inc(b2_added, 1)
                dve.wait_ge(b2_added, g + 1)

            LINKS = 3 + 14

            def group(g, attention, chain):
                a = g + 1
                slots = {5: lambda: add_b2(g)}
                if attention:
                    slots.update({-1: lambda: first_norm(a), 4: lambda: mask_and_max(a, chain),
                                  9: lambda: residual_and_norm(a, chain), 11: lambda: second_norm(a),
                                  13: lambda: x_lo_part(a)})
                slots[0] = lambda: gate(g, chain)
                slots.get(-1, lambda: None)()
                for e in range(E):
                    if e < E - 1:
                        hidden_lo(g, e + 1)
                    elif attention:
                        hidden_lo(g + 1, 0)
                    slots.get(2 * e, lambda: None)()
                    add_expert(g, e)
                    slots.get(2 * e + 1, lambda: None)()

            dve.sem_inc(hlo_ready, LO_CREDIT)
            dve.sem_inc(y_used, YF_CREDIT)
            chain = Chain(dve, dve_chain)
            dve.wait_ge(x_in[0], 16)
            first_norm_stats(0, TG, chain)
            dve.wait_ge(rstd_ready, 1)
            first_norm(0)
            dve.wait_ge(small_in, 16 * 5)
            dve.wait_ge(const_ready, 4)
            nc.vector.tensor_scalar(gate_hi[:, :], gate_sb[:, :], SW, None, ALU.mult)
            rows = [slice(32 * q, 32 * q + E) for q in range(3)]
            for r in rows:
                last = nc.vector.tensor_scalar(b2_cat[r, :], b2_rows[r, :], SW, None, ALU.mult)
            last.then_inc(small_hi, 1)
            dve.wait_ge(small_hi, 1)
            nc.vector.scalar_tensor_tensor(out=gate_lo[:, :], in0=gate_sb[:, :], scalar=SW, in1=gate_hi[:, :],
                                           op0=ALU.mult, op1=ALU.subtract)
            nc.vector.scalar_tensor_tensor(out=b2_cat[rows[2], :], in0=b2_rows[rows[2], :], scalar=SW,
                                           in1=b2_cat[rows[2], :], op0=ALU.mult,
                                           op1=ALU.subtract).then_inc(small_lo, 1)

            def weight_lo(e):
                dve.wait_ge(whi_ready, e + 1)
                nc.vector.scalar_tensor_tensor(out=w1_lo[:, e, :], in0=w1_sb[:, e, :], scalar=SW, in1=w1_hi[:, e, :],
                                               op0=ALU.mult, op1=ALU.subtract)
                nc.vector.scalar_tensor_tensor(out=w2_lo[:, e, :, :], in0=w2_sb[:, e, :, :], scalar=SW,
                                               in1=w2_hi[:, e, :, :], op0=ALU.mult,
                                               op1=ALU.subtract).then_inc(wlo_ready, 1)

            mask_and_max(0, chain)
            weight_lo(0)
            weight_lo(1)
            residual_and_norm(0, chain)
            second_norm(0)
            weight_lo(2)
            x_lo_part(0)
            weight_lo(3)
            dve.wait_ge(x_in[1], 16)
            first_norm_stats(TG, TILES, chain)
            for e in range(4, E):
                weight_lo(e)
            dve.wait_ge(rstd_ready, 2)
            hidden_lo(0, 0)
            LINKS_BEFORE = chain.count
            for g in range(0, GROUPS - 1):
                inner = Chain(dve, dve_chain, LINKS_BEFORE + g * LINKS)
                group(g, True, inner)
                assert inner.count == LINKS, inner.count
            group(GROUPS - 1, False, Chain(dve, dve_chain, LINKS_BEFORE + (GROUPS - 1) * LINKS))


_INS = ['x', 'ctx_1024', 'L0_xattn_Wq', 'L0_ffn_gate_W', 'L0_ffn_W1', 'L0_ffn_b1', 'L0_ffn_W2', 'L0_ffn_b2']
_OUTS = [((32, 64, 128), 'float32')]


def kernel(**inputs):
    import numpy as _np
    import concourse.bacc as _bacc
    from concourse import mybir as _mybir
    from concourse.bass_utils import run_bass_kernel_spmd as _run

    nc = _bacc.Bacc("TRN2", target_bir_lowering=False, num_devices=1)
    arrays, args = {}, []
    for name in _INS:
        a = _np.ascontiguousarray(inputs[name])
        arrays[f"in_{name}_dram"] = a
        args.append(nc.dram_tensor(f"in_{name}_dram", a.shape, _mybir.dt.from_np(a.dtype), kind="ExternalInput").ap())
    for i, (shape, dtype) in enumerate(_OUTS):
        dt = _mybir.dt.from_np(_np.dtype(dtype))
        args.append(nc.dram_tensor(f"out_{i}_dram", shape, dt, kind="ExternalOutput").ap())
    xattn_moe(nc, *args)
    r = _run(nc, [arrays], core_ids=[0])
    return r.results[0]["out_0_dram"]
```

```python
import concourse.bass as bass
from concourse import mybir
from contextlib import ExitStack

fp32 = mybir.dt.float32
fp16 = mybir.dt.float16
i32 = mybir.dt.int32
ALU = mybir.AluOpType
ACT = mybir.ActivationFunctionType
AX = mybir.AxisListType


class Chain:

    def __init__(self, engine, semaphore, base=0):
        self.engine, self.semaphore, self.base, self.count = engine, semaphore, base, 0

    def mark(self, instruction):
        instruction.then_inc(self.semaphore, 1)
        self.count += 1

    def wait(self):
        self.engine.wait_ge(self.semaphore, self.base + self.count)

    def link(self, instruction, meanwhile=None):
        self.mark(instruction)
        if meanwhile:
            meanwhile()
        self.wait()


def xattn_moe(nc, x, ctx, wq, gate_w, w1, b1, w2, b2, out):
    P = 128
    BATCH, SEQ, D = x.shape
    E, _, HID = w1.shape
    TOKENS = BATCH * SEQ
    TILES = TOKENS // P
    TG = 4
    GROUPS = TILES // TG
    GT = TG * P
    C = HID // P
    EPS = 1e-5
    SCALE = float(D) ** -0.5
    MASKED = 1e30
    SX, SW, SH = 16.0, 64.0, 16.0
    HB = 2 * C
    Y_FREE = 2
    SPLIT = [e % 2 == 0 for e in range(E)]
    NSPLIT = sum(SPLIT)
    PAIRS = E // 2
    NB2 = 3 * 32

    x_v = x.rearrange("b s d -> (b s) d").rearrange("(t p) d -> p t d", p=P)
    ctx_v = ctx.rearrange("b s d -> (b s) d").rearrange("(t p) d -> p t d", p=P)
    out_v = out.rearrange("b s d -> (b s) d").rearrange("(t p) d -> p t d", p=P)
    w1_v = w1.rearrange("e d h -> d e h")
    w2_v = w2.rearrange("e (c p) n -> p e c n", p=P)

    def splits(g, e):
        return g * NSPLIT + sum(SPLIT[0:e + 1])

    stack = ExitStack()
    with stack:
        def sb(name, shape, dt=fp32):
            return stack.enter_context(nc.sbuf_tensor(name, shape, dt))

        def bank(name):
            return stack.enter_context(nc.psum_tensor(name, [P, 512], fp32))

        def sem(name):
            return stack.enter_context(nc.semaphore(name))

        x_sb = sb("x_sb", [P, TILES, D])
        ctx_sb = sb("ctx_sb", [P, TG, D])
        wq_sb = sb("wq_sb", [P, D])
        gate_sb = sb("gate_sb", [P, E])
        b1_rows = sb("b1_rows", [E * C, P])
        b2_rows = sb("b2_rows", [NB2, D])
        w1_sb = sb("w1_sb", [P, E, HID])
        w2_sb = sb("w2_sb", [P, E, C, D])
        ident = sb("ident", [P, P])
        ident16 = sb("ident16", [P, P], fp16)
        mask = sb("mask", [P, P])
        restart = sb("restart", [P, TG, E])
        half = sb("half", [P, TILES])
        gram = sb("gram", [P, D])
        wqT = sb("wqT", [P, D])
        b1T = sb("b1T", [P, 2, E * C])
        w1_hi = sb("w1_hi", [P, E, HID], fp16)
        w1_lo = sb("w1_lo", [P, E, HID], fp16)
        w2_hi = sb("w2_hi", [P, E, C, D], fp16)
        w2_lo = sb("w2_lo", [P, E, C, D], fp16)
        gate_hi = sb("gate_hi", [P, E], fp16)
        gate_lo = sb("gate_lo", [P, E], fp16)
        b2_cat = sb("b2_cat", [NB2, D], fp16)
        stats = sb("stats", [P, TILES, 6])
        mv = sb("mv", [P, TILES, 2])
        rstd = sb("rstd", [P, TILES])
        xn = sb("xn", [P, TG, D])
        xnT = sb("xnT", [P, TG, P])
        ctxT = sb("ctxT", [P, TG, P])
        gT = sb("gT", [P, TG, P])
        neg_s = sb("neg_s", [P, TG, P])
        neg_max = sb("neg_max", [P, TG])
        probs = sb("probs", [P, TG, P])
        row_sum = sb("row_sum", [P, TG])
        inv_sum = sb("inv_sum", [P, TG])
        probsT = sb("probsT", [P, TG, P])
        uT = sb("uT", [P, TG, P])
        x1 = sb("x1", [P, TG, D])
        stats2 = sb("stats2", [P, TG, 6])
        mv2 = sb("mv2", [P, TG, 2])
        var2 = sb("var2", [P, TG])
        rstd2 = sb("rstd2", [P, TG])
        xf = sb("xf", [P, TG, D])
        logits = sb("logits", [P, TG, E])
        top8 = sb("top8", [P, TG, 8])
        below = sb("below", [P, TG, E])
        gate_exp = sb("gate_exp", [P, TG, E])
        is_second = sb("is_second", [P, TG, E])
        nth = sb("nth", [P, TG, E])
        one_above = sb("one_above", [P, TG])
        above = sb("above", [P, TG, E])
        chosen = sb("chosen", [P, TG, E])
        sum_two = sb("sum_two", [P, TG])
        sum_all = sb("sum_all", [P, TG])
        inv_two = sb("inv_two", [P, TG])
        weight = sb("weight", [P, TG, E])
        weight_y = sb("weight_y", [P, TG, E])
        weight_cat = sb("weight_cat", [P, TG, NB2], fp16)
        weight_catT = sb("weight_catT", [NB2, TG, P], fp16)
        x_hi = sb("x_hi", [P, GROUPS, GT], fp16)
        x_lo = sb("x_lo", [P, GROUPS, GT], fp16)
        h = sb("h", [P, HB, GT])
        h_hi = sb("h_hi", [P, C, GT], fp16)
        h_lo = sb("h_lo", [P, C, GT], fp16)
        acc = sb("acc", [P, TILES, D])

        psA, psB, psC, psD = (bank(f"ps{c}") for c in "ABCD")
        psH = [bank(f"psH{i}") for i in range(2)]
        psY = [bank(f"psY{i}") for i in range(2)]

        wq_in, small_in = sem("wq_in"), sem("small_in")
        x_in, ctx_in = [sem("x_in0"), sem("x_in_rest")], sem("ctx_in")
        w1_in = [sem(f"w1_in{p}") for p in range(PAIRS)]
        w2_in = [sem(f"w2_in{p}") for p in range(PAIRS)]
        out_done = sem("out_done")
        const_zero, const_ready = sem("const_zero"), sem("const_ready")
        prep_ps, gram_ready, wqT_ready = sem("prep_ps"), sem("gram_ready"), sem("wqT_ready")
        b1_ready, small_hi, small_lo = sem("b1_ready"), sem("small_hi"), sem("small_lo")
        w1hi_ready, w1lo_ready = sem("w1hi_ready"), sem("w1lo_ready")
        w2hi_ready, w2lo_ready = sem("w2hi_ready"), sem("w2lo_ready")
        var_ready, rstd_ready, xn_ready = sem("var_ready"), sem("rstd_ready"), sem("xn_ready")
        xnT_ps, xnT_ready, ctxT_ps, ctxT_ready = sem("xnT_ps"), sem("xnT_ready"), sem("ctxT_ps"), sem("ctxT_ready")
        gT_ps, gT_ready, scores_ps, neg_ready = sem("gT_ps"), sem("gT_ready"), sem("scores_ps"), sem("neg_ready")
        probs_ready, probsT_ps, probsT_ready = sem("probs_ready"), sem("probsT_ps"), sem("probsT_ready")
        uT_ps, uT_ready, attn_ps = sem("uT_ps"), sem("uT_ready"), sem("attn_ps")
        x1_ready, var2_ready, rstd2_ready = sem("x1_ready"), sem("var2_ready"), sem("rstd2_ready")
        xf_ready, xfT_ps, xhi_ready, xlo_ready = sem("xf_ready"), sem("xfT_ps"), sem("xhi_ready"), sem("xlo_ready")
        base_ready = sem("base_ready")
        logits_ps, below_ready, gate_exp_ready = sem("logits_ps"), sem("below_ready"), sem("gate_exp_ready")
        cat_ready, catT_ps, catT_ready, b2_ps, b2_added = (
            sem("cat_ready"), sem("catT_ps"), sem("catT_ready"), sem("b2_ps"), sem("b2_added"))
        z_ps, h_ready, hlo_ready = sem("z_ps"), sem("h_ready"), sem("hlo_ready")
        y_ps, y_used = sem("y_ps"), sem("y_used")
        dve_chain = sem("dve_chain")

        block = stack.enter_context(nc.Block())

        def tiles(t):
            return t[:, :].rearrange("p (t n) -> p t n", n=P)

        CAT_T, B2_PRODUCT, B2_ADD = 3, 4, 5
        XN_T, GRAM, SCORES, MAX, EXPS, PROBS_T, CONTEXT, VALUES = 1, 2, 3, 3, 4, 5, 6, 8
        RESIDUAL, NORM2, XF_T, X_LO, LOGITS, GATE_TOP = 8, 9, 11, 12, 14, 14

        def run(steps, slot):
            for at, step in steps:
                if at == slot:
                    step()

        def over(ap, n):
            return ap.unsqueeze(2).broadcast_to([P, TG, n])

        @block.sync
        def _(sp):
            sp.dma_start(x_sb[:, 0:TG, :], x_v[:, 0:TG, :]).then_inc(x_in[0], 16)
            sp.dma_start(ctx_sb[:, :, :], ctx_v[:, 0:TG, :]).then_inc(ctx_in, 16)

            def weights(p):
                e = slice(2 * p, 2 * p + 2)
                sp.dma_start(w1_sb[:, e, :], w1_v[:, e, :]).then_inc(w1_in[p], 16)
                for i in range(2 * p, 2 * p + 2):
                    sp.dma_start(w2_sb[:, i, :, :], w2_v[:, i, :, :]).then_inc(w2_in[p], 16)

            weights(0)
            weights(1)
            sp.dma_start(x_sb[:, TG:, :], x_v[:, TG:, :]).then_inc(x_in[1], 16)
            weights(2)
            weights(3)

            def next_context(a):
                sp.wait_ge(uT_ps, a)
                sp.dma_start(ctx_sb[:, :, :], ctx_v[:, bass.ts(a, TG), :]).then_inc(ctx_in, 16)

            def store(g):
                sp.wait_ge(y_used, Y_FREE + (g + 1) * E)
                sp.dma_start(out_v[:, bass.ts(g, TG), :], acc[:, bass.ts(g, TG), :]).then_inc(out_done, 16)

            next_context(1)
            for g in range(0, GROUPS - 2):
                next_context(g + 2)
                store(g)
            store(GROUPS - 2)
            store(GROUPS - 1)
            sp.wait_ge(out_done, 16 * GROUPS)

        @block.tensor
        def _(pe):
            def transposes(bank_ap, src, ready, wait):
                for t in range(TG):
                    wait(t)
                    last = nc.tensor.transpose(bank_ap[:, t, :], src[:, t, :], ident[:, :])
                last.then_inc(ready, 1)

            def xn_ctx_transposes(a, first=False):
                transposes(tiles(psA), xn, xnT_ps, lambda t: pe.wait_ge(xn_ready, a * TG + t + 1))
                pe.wait_ge(ctx_in, 16 * (a + 1))
                if not first:
                    pe.wait_ge(below_ready, a)
                transposes(tiles(psB), ctx_sb, ctxT_ps, lambda t: None)

            def gram_product(a):
                pe.wait_ge(xnT_ready, a + 1)
                nc.tensor.matmul(psC[:, :], gram[:, :], xnT[:, :, :], start=True, stop=True).then_inc(gT_ps, 1)

            def score_product(a):
                pe.wait_ge(gT_ready, a + 1)
                pe.wait_ge(ctxT_ready, a + 1)
                for t in range(TG):
                    last = nc.tensor.matmul(tiles(psA)[:, t, :], gT[:, t, :], ctxT[:, t, :], start=True, stop=True)
                last.then_inc(scores_ps, 1)

            def probs_transposes(a):
                transposes(tiles(psB), probs, probsT_ps, lambda t: pe.wait_ge(probs_ready, a * TG + t + 1))

            def context_product(a):
                pe.wait_ge(probsT_ready, a + 1)
                for t in range(TG):
                    last = nc.tensor.matmul(tiles(psC)[:, t, :], ctx_sb[:, t, :], probsT[:, t, :],
                                            start=True, stop=True)
                last.then_inc(uT_ps, 1)

            def value_product(a, first):
                pe.wait_ge(uT_ready, a + 1)
                if not first:
                    pe.wait_ge(b2_added, a)
                for t in range(TG):
                    last = nc.tensor.matmul(tiles(psD)[:, t, :], uT[:, t, :], wqT[:, :], start=True, stop=True)
                last.then_inc(attn_ps, 1)

            def xf_transposes(a):
                transposes(tiles(psA), xf, xfT_ps, lambda t: pe.wait_ge(xf_ready, a * TG + t + 1))

            def logit_product(a):
                pe.wait_ge(xlo_ready, a + 1)
                for t in range(TG):
                    o = psB[:, t * E:(t + 1) * E]
                    hi, lo = (v[:, a, t * P:(t + 1) * P] for v in (x_hi, x_lo))
                    nc.tensor.matmul(o, hi, gate_hi[:, :], start=True, stop=False)
                    nc.tensor.matmul(o, hi, gate_lo[:, :], start=False, stop=False)
                    last = nc.tensor.matmul(o, lo, gate_hi[:, :], start=False, stop=True)
                last.then_inc(logits_ps, 1)

            cat_ps = psD[0:NB2, 0:TG * P // 2].bitcast(fp16).rearrange("p (t n) -> p t n", n=P)

            def cat_transposes(g):
                pe.wait_ge(cat_ready, g + 1)
                for t in range(TG):
                    last = nc.tensor.transpose(cat_ps[:, t, :], weight_cat[:, t, :], ident16[:, :])
                last.then_inc(catT_ps, 1)

            def b2_product(g):
                pe.wait_ge(catT_ready, g + 1)
                for t in range(TG):
                    last = nc.tensor.matmul(tiles(psD)[:, t, :], weight_catT[:, t, :], b2_cat[:, :],
                                            start=True, stop=True)
                last.then_inc(b2_ps, 1)

            def hidden_product(g, e, first=False):
                u = (g * E + e) * C
                if e == 0:
                    pe.wait_ge(xlo_ready, g + 1)
                pe.wait_ge(w1lo_ready, e // 2 + 1)
                for c in range(C):
                    if not first:
                        pe.wait_ge(h_ready, u + c - 1)
                    w = slice(c * P, (c + 1) * P)
                    nc.tensor.matmul(psH[c][:, :], w1_hi[:, e, w], x_hi[:, g, :], start=True, stop=False)
                    nc.tensor.matmul(psH[c][:, :], w1_hi[:, e, w], x_lo[:, g, :], start=False, stop=False)
                    nc.tensor.matmul(psH[c][:, :], w1_lo[:, e, w], x_hi[:, g, :], start=False,
                                     stop=True).then_inc(z_ps, 1)

            def output_product(g, e):
                n = g * E + e
                i = e % 2
                if SPLIT[e]:
                    pe.wait_ge(w2lo_ready, splits(0, e))
                    pe.wait_ge(hlo_ready, splits(g, e))
                else:
                    pe.wait_ge(w2_in[e // 2], 32)
                    pe.wait_ge(h_ready, (n + 1) * C)
                pe.wait_ge(y_used, n + 1)
                for t in range(TG):
                    o = tiles(psY[i])[:, t, :]
                    tok = slice(t * P, (t + 1) * P)
                    for c in range(C):
                        first, final = c == 0, c == C - 1
                        if SPLIT[e]:
                            nc.tensor.matmul(o, h_hi[:, c, tok], w2_hi[:, e, c, :], start=first, stop=False)
                            nc.tensor.matmul(o, h_hi[:, c, tok], w2_lo[:, e, c, :], start=False, stop=False)
                            last = nc.tensor.matmul(o, h_lo[:, c, tok], w2_hi[:, e, c, :], start=False, stop=final)
                        else:
                            last = nc.tensor.matmul(o, h[:, C * i + c, tok], w2_sb[:, e, c, :], start=first,
                                                    stop=final)
                last.then_inc(y_ps, 1)

            def group(g, attention):
                a = g + 1
                steps = [(CAT_T, lambda: cat_transposes(g)), (B2_PRODUCT, lambda: b2_product(g))]
                if attention:
                    steps += [(XN_T, lambda: xn_ctx_transposes(a)), (GRAM, lambda: gram_product(a)),
                              (SCORES, lambda: score_product(a)), (PROBS_T, lambda: probs_transposes(a)),
                              (CONTEXT, lambda: context_product(a)), (VALUES, lambda: value_product(a, False)),
                              (XF_T, lambda: xf_transposes(a)), (LOGITS, lambda: logit_product(a))]
                for e in range(E):
                    if e < E - 1:
                        hidden_product(g, e + 1)
                    elif attention:
                        hidden_product(g + 1, 0)
                    run(steps, 2 * e)
                    output_product(g, e)
                    run(steps, 2 * e + 1)

            pe.wait_ge(const_ready, 1)
            pe.wait_ge(wq_in, 16)
            nc.tensor.matmul(psC[:, 0:D], wq_sb[:, :], wq_sb[:, :], start=True, stop=True)
            nc.tensor.transpose(psC[:, D:2 * D], wq_sb[:, :], ident[:, :]).then_inc(prep_ps, 1)
            pe.wait_ge(small_in, 16 * 5)
            nc.tensor.transpose(psD[:, 0:E * C], b1_rows[:, :], ident[0:E * C, 0:E * C]).then_inc(prep_ps, 1)
            xn_ctx_transposes(0, first=True)
            pe.wait_ge(wqT_ready, 1)
            gram_product(0)
            score_product(0)
            probs_transposes(0)
            context_product(0)
            pe.wait_ge(b1_ready, 1)
            value_product(0, True)
            xf_transposes(0)
            hidden_product(0, 0, first=True)
            pe.wait_ge(small_lo, 1)
            logit_product(0)
            for g in range(0, GROUPS - 1):
                group(g, True)
            group(GROUPS - 1, False)

        @block.scalar
        def _(act):
            def copy(dst, src, ready, scale=1.0):
                nc.scalar.activation(dst, src, ACT.Copy, scale=scale).then_inc(ready, 1)

            def transposed(a):
                act.wait_ge(xnT_ps, a + 1)
                copy(xnT[:, :, :], tiles(psA), xnT_ready)
                act.wait_ge(ctxT_ps, a + 1)
                copy(ctxT[:, :, :], tiles(psB), ctxT_ready)

            def gram_out(a):
                act.wait_ge(gT_ps, a + 1)
                copy(gT[:, :, :], tiles(psC), gT_ready)

            def softmax(a):
                for t in range(TG):
                    act.wait_ge(neg_ready, a * TG + t + 1)
                    nc.scalar.activation(probs[:, t, :], neg_s[:, t, :], ACT.Exp, bias=neg_max[:, t:t + 1],
                                         scale=-1.0, accum_out=row_sum[:, t:t + 1]).then_inc(probs_ready, 1)

            def probs_out(a):
                act.wait_ge(probsT_ps, a + 1)
                copy(probsT[:, :, :], tiles(psB), probsT_ready)

            def context_out(a):
                act.wait_ge(uT_ps, a + 1)
                copy(uT[:, :, :], tiles(psC), uT_ready)

            def x_hi_part(a):
                act.wait_ge(xfT_ps, a + 1)
                copy(x_hi[:, a, :], psA[:, :], xhi_ready, scale=SX)

            def gate_exps(a):
                act.wait_ge(below_ready, a + 1)
                nc.scalar.activation(gate_exp[:, :, :], below[:, :, :], ACT.Exp).then_inc(gate_exp_ready, 1)

            cat_ps = psD[0:NB2, 0:TG * P // 2].bitcast(fp16).rearrange("p (t n) -> p t n", n=P)

            def cat_out(g):
                act.wait_ge(catT_ps, g + 1)
                copy(weight_catT[:, :, :], cat_ps, catT_ready)

            def hidden_relu(g, e):
                n = g * E + e
                for c in range(C):
                    act.wait_ge(z_ps, n * C + c + 1)
                    scale = SH / (SX * SW) if SPLIT[e] else 1.0
                    bias = b1T[:, int(SPLIT[e]), e * C + c:e * C + c + 1]
                    if SPLIT[e]:
                        nc.scalar.activation(h_hi[:, c, :], psH[c][:, :], ACT.Relu, bias=bias, scale=scale)
                    nc.scalar.activation(h[:, C * (e % 2) + c, :], psH[c][:, :], ACT.Relu, bias=bias,
                                         scale=scale).then_inc(h_ready, 1)

            def group(g, attention):
                a = g + 1
                steps = [(CAT_T, lambda: cat_out(g))]
                if attention:
                    steps += [(XN_T, lambda: transposed(a)), (GRAM, lambda: gram_out(a)),
                              (EXPS, lambda: softmax(a)), (PROBS_T, lambda: probs_out(a)),
                              (CONTEXT, lambda: context_out(a)), (XF_T, lambda: x_hi_part(a)),
                              (GATE_TOP, lambda: gate_exps(a))]
                for e in range(E):
                    if e < E - 1:
                        hidden_relu(g, e + 1)
                    elif attention:
                        hidden_relu(g + 1, 0)
                    run(steps, 2 * e)
                    run(steps, 2 * e + 1)

            act.dma_start(wq_sb[:, :], wq).then_inc(wq_in, 16)
            act.dma_start(gate_sb[:, :], gate_w).then_inc(small_in, 16)
            act.dma_start(b1_rows[:, :], b1.rearrange("e (c p) -> (e c) p", p=P)).then_inc(small_in, 16)
            for q in range(3):
                act.dma_start(b2_rows[32 * q:32 * q + E, :], b2).then_inc(small_in, 16)

            def w1_hi_part(p):
                act.wait_ge(w1_in[p], 16)
                copy(w1_hi[:, 2 * p:2 * p + 2, :], w1_sb[:, 2 * p:2 * p + 2, :], w1hi_ready, scale=SW)

            def w2_hi_part(e):
                act.wait_ge(w2_in[e // 2], 32)
                copy(w2_hi[:, e, :, :], w2_sb[:, e, :, :], w2hi_ready, scale=SW)

            act.wait_ge(prep_ps, 1)
            copy(gram[:, :], psC[:, 0:D], gram_ready, scale=-SCALE)
            copy(wqT[:, :], psC[:, D:2 * D], wqT_ready)
            act.wait_ge(prep_ps, 2)
            nc.scalar.activation(b1T[:, 0, :], psD[:, 0:E * C], ACT.Copy, scale=SX * SW)
            copy(b1T[:, 1, :], psD[:, 0:E * C], b1_ready, scale=SH)
            act.wait_ge(b1_ready, 1)
            transposed(0)
            gram_out(0)
            w1_hi_part(0)
            w2_hi_part(0)
            w1_hi_part(1)
            softmax(0)
            probs_out(0)
            w2_hi_part(2)
            context_out(0)
            w1_hi_part(2)
            w2_hi_part(4)
            w1_hi_part(3)
            w2_hi_part(6)
            x_hi_part(0)
            hidden_relu(0, 0)
            gate_exps(0)
            for g in range(0, GROUPS - 1):
                group(g, True)
            group(GROUPS - 1, False)

        @block.gpsimd
        def _(pool):
            nc.gpsimd.memset(ident[:, :], 0.0).then_inc(const_zero, 1)
            nc.gpsimd.memset(ident16[:, :], 0.0).then_inc(const_zero, 1)
            nc.gpsimd.memset(mask[:, :], 0.0).then_inc(const_zero, 1)
            pool.wait_ge(const_zero, 3)
            nc.gpsimd.affine_select(out=ident[:, :], in_=ident[:, :], compare_op=ALU.not_equal, fill=1.0, base=0,
                                    pattern=[[-1, P]], channel_multiplier=1).then_inc(const_ready, 1)
            nc.gpsimd.affine_select(out=ident16[:, :], in_=ident16[:, :], compare_op=ALU.not_equal, fill=1.0,
                                    base=0, pattern=[[-1, P]], channel_multiplier=1).then_inc(const_zero, 1)
            nc.gpsimd.affine_select(out=mask[:, :], in_=mask[:, :], compare_op=ALU.is_ge, fill=MASKED, base=0,
                                    pattern=[[-1, P]], channel_multiplier=1).then_inc(const_zero, 1)
            pool.wait_ge(const_zero, 5)
            nc.gpsimd.memset(mask[SEQ:P, 0:SEQ], MASKED).then_inc(const_zero, 1)
            pool.wait_ge(const_zero, 6)
            nc.gpsimd.memset(restart[:, :, :], 1.0).then_inc(const_zero, 1)
            pool.wait_ge(const_zero, 7)
            nc.gpsimd.memset(restart[:, :, 0:1], 0.0)
            nc.gpsimd.memset(half[:, :], -0.5).then_inc(const_ready, 1)
            nc.gpsimd.memset(weight_cat[:, :, :], 0.0).then_inc(const_ready, 1)
            nc.gpsimd.memset(b2_cat[:, :], 0.0).then_inc(const_ready, 1)
            pool.wait_ge(const_ready, 4)

            def inv_std(dst, var, n, ready):
                nc.gpsimd.tensor_tensor(dst, var, half[:, 0:n], ALU.pow).then_inc(ready, 1)

            def attention_rstd(a):
                pool.wait_ge(var2_ready, a + 1)
                inv_std(rstd2[:, :], var2[:, :], TG, rstd2_ready)

            def base_sum(a):
                pool.wait_ge(xf_ready, (a + 1) * TG)
                nc.gpsimd.tensor_tensor(acc[:, bass.ts(a, TG), :], x1[:, :, :], xf[:, :, :],
                                        ALU.add).then_inc(base_ready, 1)

            pool.wait_ge(var_ready, 1)
            inv_std(rstd[:, 0:TG], mv[:, 0:TG, 1], TG, rstd_ready)
            attention_rstd(0)
            base_sum(0)
            pool.wait_ge(var_ready, 2)
            inv_std(rstd[:, TG:], mv[:, TG:, 1], TILES - TG, rstd_ready)
            for g in range(0, GROUPS - 1):
                attention_rstd(g + 1)
                base_sum(g + 1)

        @block.vector
        def _(dve):
            def first_norm_stats(t0, t1, chain):
                for t in range(t0, t1):
                    last = nc.vector.bn_stats(stats[:, t, :], x_sb[:, t, :])
                chain.link(last)
                for t in range(t0, t1):
                    last = nc.vector.bn_aggr(mv[:, t, :], stats[:, t, :])
                chain.link(last)
                nc.vector.tensor_scalar(mv[:, t0:t1, 1], mv[:, t0:t1, 1], EPS, None, ALU.add).then_inc(var_ready, 1)

            def first_norm(g, t):
                i = g * TG + t
                nc.vector.tensor_scalar(xn[:, t, :], x_sb[:, i, :], mv[:, i, 0:1], rstd[:, bass.ds(i, 1)],
                                        ALU.subtract, ALU.mult).then_inc(xn_ready, 1)

            def mask_and_max(a):
                dve.wait_ge(scores_ps, a + 1)
                for t in range(TG):
                    nc.vector.tensor_tensor_reduce(
                        out=neg_s[:, t, :], in0=tiles(psA)[:, t, :], in1=mask[:, :], scale=1.0, scalar=3e38,
                        op0=ALU.add, op1=ALU.min, accum_out=neg_max[:, t:t + 1]).then_inc(neg_ready, 1)

            def residual_and_norm(a, chain):
                dve.wait_ge(probs_ready, (a + 1) * TG)
                chain.link(nc.vector.reciprocal(inv_sum[:, :], row_sum[:, :]))
                dve.wait_ge(attn_ps, a + 1)
                for t in range(TG):
                    last = nc.vector.scalar_tensor_tensor(
                        out=x1[:, t, :], in0=tiles(psD)[:, t, :], scalar=inv_sum[:, t:t + 1],
                        in1=x_sb[:, a * TG + t, :], op0=ALU.mult, op1=ALU.add)
                chain.link(last)
                for t in range(TG):
                    last = nc.vector.bn_stats(stats2[:, t, :], x1[:, t, :])
                chain.link(last)
                for t in range(TG):
                    last = nc.vector.bn_aggr(mv2[:, t, :], stats2[:, t, :])
                chain.link(last)
                nc.vector.tensor_scalar(var2[:, :], mv2[:, :, 1], EPS, None, ALU.add).then_inc(var2_ready, 1)

            def second_norm(a):
                dve.wait_ge(rstd2_ready, a + 1)
                for t in range(TG):
                    nc.vector.tensor_scalar(xf[:, t, :], x1[:, t, :], mv2[:, t, 0:1], rstd2[:, t:t + 1],
                                            ALU.subtract, ALU.mult).then_inc(xf_ready, 1)

            def x_lo_part(a):
                dve.wait_ge(xhi_ready, a + 1)
                nc.vector.scalar_tensor_tensor(out=x_lo[:, a, :], in0=psA[:, :], scalar=SX, in1=x_hi[:, a, :],
                                               op0=ALU.mult, op1=ALU.subtract).then_inc(xlo_ready, 1)

            first, second = top8[:, :, 0], top8[:, :, 1]
            TT = nc.vector.tensor_tensor

            def gate_top(a, chain):
                dve.wait_ge(logits_ps, a + 1)
                chain.link(nc.vector.tensor_scalar(logits[:, :, :], psB[:, 0:TG * E].rearrange("p (t e) -> p t e", e=E),
                                                   1.0 / (SX * SW), None, ALU.mult))
                for t in range(TG):
                    last = nc.vector.max(top8[:, t, :], logits[:, t, :])
                chain.link(last)
                TT(below[:, :, :], logits[:, :, :], over(first, E), ALU.subtract).then_inc(below_ready, 1)
                TT(is_second[:, :, :], logits[:, :, :], over(second, E), ALU.is_equal)
                TT(one_above[:, :], first, second, ALU.is_gt)
                chain.link(TT(above[:, :, :], logits[:, :, :], over(second, E), ALU.is_gt))

            def gate_choice(a, chain, meanwhile):
                between = meanwhile or [None] * 4
                chain.link(nc.vector.tensor_tensor_scan(
                    nth[:, :, :].rearrange("p t e -> p (t e)"), restart[:, :, :].rearrange("p t e -> p (t e)"),
                    is_second[:, :, :].rearrange("p t e -> p (t e)"), 0.0, ALU.mult, ALU.add), between[0])
                chain.link(TT(nth[:, :, :], nth[:, :, :], over(one_above[:, :], E), ALU.add), between[1])
                chain.link(nc.vector.scalar_tensor_tensor(out=chosen[:, :, :], in0=nth[:, :, :], scalar=2.0,
                                                          in1=is_second[:, :, :], op0=ALU.is_le, op1=ALU.mult),
                           between[2])
                chain.link(TT(chosen[:, :, :], chosen[:, :, :], above[:, :, :], ALU.add), between[3])

            def gate_weights(a, chain):
                dve.wait_ge(gate_exp_ready, a + 1)
                chain.link(TT(chosen[:, :, :], chosen[:, :, :], gate_exp[:, :, :], ALU.mult))
                nc.vector.reduce_sum(sum_two[:, :], chosen[:, :, :], axis=AX.X)
                chain.link(nc.vector.reduce_sum(sum_all[:, :], gate_exp[:, :, :], axis=AX.X))
                chain.link(nc.vector.scalar_tensor_tensor(out=sum_two[:, :], in0=sum_all[:, :], scalar=1e-8,
                                                          in1=sum_two[:, :], op0=ALU.mult, op1=ALU.add))
                chain.link(nc.vector.reciprocal(inv_two[:, :], sum_two[:, :]))
                chain.link(TT(weight[:, :, :], chosen[:, :, :], over(inv_two[:, :], E), ALU.mult))
                dve.wait_ge(y_used, Y_FREE + a * E)
                nc.vector.tensor_scalar(weight_y[:, :, :], weight[:, :, :], 1.0 / (SH * SW), None, ALU.mult)
                nc.vector.tensor_scalar(weight_cat[:, :, 64:64 + E], weight[:, :, :], SX, None, ALU.mult)
                chain.link(nc.vector.tensor_scalar(weight_cat[:, :, 0:E], weight[:, :, :], SX, None, ALU.mult))
                nc.vector.scalar_tensor_tensor(out=weight_cat[:, :, 32:32 + E], in0=weight[:, :, :], scalar=SX,
                                               in1=weight_cat[:, :, 0:E], op0=ALU.mult,
                                               op1=ALU.subtract).then_inc(cat_ready, 1)
                dve.wait_ge(cat_ready, a + 1)

            def hidden_lo(g, e):
                if SPLIT[e]:
                    dve.wait_ge(h_ready, (g * E + e + 1) * C)
                    nc.vector.tensor_tensor(h_lo[:, :, :], h[:, C * (e % 2):C * (e % 2 + 1), :], h_hi[:, :, :],
                                            ALU.subtract).then_inc(hlo_ready, 1)

            def add_expert(g, e, last_expert=False):
                n = g * E + e
                dve.wait_ge(y_ps, n + 1)
                if e == 0:
                    dve.wait_ge(base_ready, g + 1)
                else:
                    dve.wait_ge(y_used, Y_FREE + n)
                for t in range(TG):
                    o = acc[:, g * TG + t, :]
                    last = nc.vector.scalar_tensor_tensor(out=o, in0=tiles(psY[e % 2])[:, t, :],
                                                          scalar=weight_y[:, t, e:e + 1], in1=o,
                                                          op0=ALU.mult, op1=ALU.add)
                last.then_inc(y_used, 1)

            def add_b2(g):
                dve.wait_ge(b2_ps, g + 1)
                dve.wait_ge(y_used, Y_FREE + g * E + 3)
                o = acc[:, bass.ts(g, TG), :]
                nc.vector.scalar_tensor_tensor(out=o, in0=tiles(psD), scalar=1.0 / (SX * SW), in1=o,
                                               op0=ALU.mult, op1=ALU.add).then_inc(b2_added, 1)
                dve.wait_ge(b2_added, g + 1)

            LINKS = 3 + 14

            def group(g, attention, chain):
                a = g + 1
                steps = [(B2_ADD, lambda: add_b2(g))]
                if attention:
                    steps += [(MAX, lambda: mask_and_max(a)), (RESIDUAL, lambda: residual_and_norm(a, chain)),
                              (NORM2, lambda: second_norm(a)), (X_LO, lambda: x_lo_part(a)),
                              (GATE_TOP, lambda: gate_top(a, chain))]
                gate_choice(g, chain, [lambda t=t: first_norm(a, t) for t in range(TG)] if attention else None)
                gate_weights(g, chain)
                for e in range(E):
                    if e < E - 1:
                        hidden_lo(g, e + 1)
                    elif attention:
                        hidden_lo(g + 1, 0)
                    run(steps, 2 * e)
                    add_expert(g, e)
                    run(steps, 2 * e + 1)

            dve.sem_inc(y_used, Y_FREE)
            chain = Chain(dve, dve_chain)
            dve.wait_ge(x_in[0], 16)
            first_norm_stats(0, TG, chain)
            dve.wait_ge(rstd_ready, 1)
            for t in range(TG):
                first_norm(0, t)
            dve.wait_ge(small_in, 16 * 5)
            dve.wait_ge(const_ready, 4)
            nc.vector.tensor_scalar(gate_hi[:, :], gate_sb[:, :], SW, None, ALU.mult)
            rows = [slice(32 * q, 32 * q + E) for q in range(3)]
            for r in rows:
                last = nc.vector.tensor_scalar(b2_cat[r, :], b2_rows[r, :], SW, None, ALU.mult)
            last.then_inc(small_hi, 1)
            dve.wait_ge(small_hi, 1)
            nc.vector.scalar_tensor_tensor(out=gate_lo[:, :], in0=gate_sb[:, :], scalar=SW, in1=gate_hi[:, :],
                                           op0=ALU.mult, op1=ALU.subtract)
            nc.vector.scalar_tensor_tensor(out=b2_cat[rows[2], :], in0=b2_rows[rows[2], :], scalar=SW,
                                           in1=b2_cat[rows[2], :], op0=ALU.mult,
                                           op1=ALU.subtract).then_inc(small_lo, 1)

            def w1_lo_part(p):
                dve.wait_ge(w1hi_ready, p + 1)
                w = (slice(None), slice(2 * p, 2 * p + 2), slice(None))
                nc.vector.scalar_tensor_tensor(out=w1_lo[w], in0=w1_sb[w], scalar=SW, in1=w1_hi[w],
                                               op0=ALU.mult, op1=ALU.subtract).then_inc(w1lo_ready, 1)

            def w2_lo_part(e):
                dve.wait_ge(w2hi_ready, splits(0, e))
                nc.vector.scalar_tensor_tensor(out=w2_lo[:, e, :, :], in0=w2_sb[:, e, :, :], scalar=SW,
                                               in1=w2_hi[:, e, :, :], op0=ALU.mult,
                                               op1=ALU.subtract).then_inc(w2lo_ready, 1)

            mask_and_max(0)
            w1_lo_part(0)
            w2_lo_part(0)
            w1_lo_part(1)
            residual_and_norm(0, chain)
            second_norm(0)
            w2_lo_part(2)
            x_lo_part(0)
            dve.wait_ge(x_in[1], 16)
            first_norm_stats(TG, TILES, chain)
            w1_lo_part(2)
            w2_lo_part(4)
            hidden_lo(0, 0)
            gate_top(0, chain)
            w1_lo_part(3)
            w2_lo_part(6)
            dve.wait_ge(rstd_ready, 2)
            LINKS_BEFORE = chain.count
            for g in range(0, GROUPS - 1):
                inner = Chain(dve, dve_chain, LINKS_BEFORE + g * LINKS)
                group(g, True, inner)
                assert inner.count == LINKS, inner.count
            group(GROUPS - 1, False, Chain(dve, dve_chain, LINKS_BEFORE + (GROUPS - 1) * LINKS))


_INS = ['x', 'ctx_1024', 'L0_xattn_Wq', 'L0_ffn_gate_W', 'L0_ffn_W1', 'L0_ffn_b1', 'L0_ffn_W2', 'L0_ffn_b2']
_OUTS = [((32, 64, 128), 'float32')]


def kernel(**inputs):
    import numpy as _np
    import concourse.bacc as _bacc
    from concourse import mybir as _mybir
    from concourse.bass_utils import run_bass_kernel_spmd as _run

    nc = _bacc.Bacc("TRN2", target_bir_lowering=False, num_devices=1)
    arrays, args = {}, []
    for name in _INS:
        a = _np.ascontiguousarray(inputs[name])
        arrays[f"in_{name}_dram"] = a
        args.append(nc.dram_tensor(f"in_{name}_dram", a.shape, _mybir.dt.from_np(a.dtype), kind="ExternalInput").ap())
    for i, (shape, dtype) in enumerate(_OUTS):
        dt = _mybir.dt.from_np(_np.dtype(dtype))
        args.append(nc.dram_tensor(f"out_{i}_dram", shape, dt, kind="ExternalOutput").ap())
    xattn_moe(nc, *args)
    r = _run(nc, [arrays], core_ids=[0])
    return r.results[0]["out_0_dram"]
```

```python
import concourse.bass as bass
from concourse import mybir
from contextlib import ExitStack

fp32 = mybir.dt.float32
fp16 = mybir.dt.float16
i32 = mybir.dt.int32
ALU = mybir.AluOpType
ACT = mybir.ActivationFunctionType
AX = mybir.AxisListType


class Chain:

    def __init__(self, engine, semaphore, base=0):
        self.engine, self.semaphore, self.base, self.count = engine, semaphore, base, 0

    def mark(self, instruction):
        instruction.then_inc(self.semaphore, 1)
        self.count += 1

    def wait(self):
        self.engine.wait_ge(self.semaphore, self.base + self.count)

    def link(self, instruction, meanwhile=None):
        self.mark(instruction)
        if meanwhile:
            meanwhile()
        self.wait()


def xattn_moe(nc, x, ctx, wq, gate_w, w1, b1, w2, b2, out):
    P = 128
    BATCH, SEQ, D = x.shape
    E, _, HID = w1.shape
    TOKENS = BATCH * SEQ
    TILES = TOKENS // P
    TG = 4
    GROUPS = TILES // TG
    GT = TG * P
    C = HID // P
    EPS = 1e-5
    SCALE = float(D) ** -0.5
    MASKED = 1e30
    SX, SW, SH = 16.0, 64.0, 16.0
    FULL = (0, 3)
    FULL_LAST = (0, 7)
    HB = 2 * C
    Y_FREE = 2
    WARM_UP = 9
    PAIRS = E // 2
    NB2 = 3 * 32

    x_v = x.rearrange("b s d -> (b s) d").rearrange("(t p) d -> p t d", p=P)
    ctx_v = ctx.rearrange("b s d -> (b s) d").rearrange("(t p) d -> p t d", p=P)
    out_v = out.rearrange("b s d -> (b s) d").rearrange("(t p) d -> p t d", p=P)
    w1_v = w1.rearrange("e d h -> d e h")
    w2_v = w2.rearrange("e (c p) n -> p (e c) n", p=P)

    def is_split(g, e):
        return e not in (FULL_LAST if isinstance(g, int) and g == GROUPS - 1 else FULL)

    def splits(g, e):
        return g * (E - len(FULL)) + sum(is_split(g, i) for i in range(e + 1))

    stack = ExitStack()
    with stack:
        def sb(name, shape, dt=fp32):
            return stack.enter_context(nc.sbuf_tensor(name, shape, dt))

        def bank(name):
            return stack.enter_context(nc.psum_tensor(name, [P, 512], fp32))

        def sem(name):
            return stack.enter_context(nc.semaphore(name))

        x_sb = sb("x_sb", [P, TILES, D])
        ctx_sb = sb("ctx_sb", [P, TG, D])
        wq_sb = sb("wq_sb", [P, D])
        gate_sb = sb("gate_sb", [P, E])
        b1_rows = sb("b1_rows", [E * C, P])
        b2_rows = sb("b2_rows", [NB2, D])
        w1_sb = sb("w1_sb", [P, E, HID])
        w2_sb = sb("w2_sb", [P, E, C, D])
        ident = sb("ident", [P, P])
        ident16 = sb("ident16", [P, P], fp16)
        mask = sb("mask", [P, P])
        restart = sb("restart", [P, TG, E])
        half = sb("half", [P, TILES])
        warm = sb("warm", [P, 4 * P], fp16)
        gram = sb("gram", [P, D])
        wqT = sb("wqT", [P, D])
        b1T = sb("b1T", [P, 2, E * C])
        w1_hi = sb("w1_hi", [P, E, HID], fp16)
        w1_lo = sb("w1_lo", [P, E, HID], fp16)
        w2_hi = sb("w2_hi", [P, E, C, D], fp16)
        w2_lo = sb("w2_lo", [P, E, C, D], fp16)
        gate_hi = sb("gate_hi", [P, E], fp16)
        gate_lo = sb("gate_lo", [P, E], fp16)
        b2_cat = sb("b2_cat", [NB2, D], fp16)
        stats = sb("stats", [P, TILES, 6])
        mv = sb("mv", [P, TILES, 2])
        rstd = sb("rstd", [P, TILES])
        xn = sb("xn", [P, TG, D])
        xnT = sb("xnT", [P, TG, P])
        ctxT = sb("ctxT", [P, TG, P])
        gT = sb("gT", [P, TG, P])
        neg_s = sb("neg_s", [P, TG, P])
        neg_max = sb("neg_max", [P, TG])
        probs = sb("probs", [P, TG, P])
        row_sum = sb("row_sum", [P, TG])
        inv_sum = sb("inv_sum", [P, TG])
        probsT = sb("probsT", [P, TG, P])
        uT = sb("uT", [P, TG, P])
        x1 = sb("x1", [P, TG, D])
        stats2 = sb("stats2", [P, TG, 6])
        mv2 = sb("mv2", [P, TG, 2])
        var2 = sb("var2", [P, TG])
        rstd2 = sb("rstd2", [P, TG])
        xf = sb("xf", [P, TG, D])
        logits = sb("logits", [P, TG, E])
        top8 = sb("top8", [P, TG, 8])
        below = sb("below", [P, TG, E])
        gate_exp = sb("gate_exp", [P, TG, E])
        is_second = sb("is_second", [P, TG, E])
        nth = sb("nth", [P, TG, E])
        one_above = sb("one_above", [P, TG])
        above = sb("above", [P, TG, E])
        chosen = sb("chosen", [P, TG, E])
        sum_two = sb("sum_two", [P, TG])
        sum_all = sb("sum_all", [P, TG])
        inv_two = sb("inv_two", [P, TG])
        weight = sb("weight", [P, TG, E])
        weight_y = sb("weight_y", [P, TG, E])
        weight_cat = sb("weight_cat", [P, TG, NB2], fp16)
        weight_catT = sb("weight_catT", [NB2, TG, P], fp16)
        x_hi = sb("x_hi", [P, GROUPS, GT], fp16)
        x_lo = sb("x_lo", [P, GROUPS, GT], fp16)
        h = sb("h", [P, HB, GT])
        h_hi = sb("h_hi", [P, HB, GT], fp16)
        h_lo = sb("h_lo", [P, HB, GT], fp16)
        acc = sb("acc", [P, TILES, D])

        psA, psB, psC, psD = (bank(f"ps{c}") for c in "ABCD")
        psH = [bank(f"psH{i}") for i in range(2)]
        psY = [bank(f"psY{i}") for i in range(2)]
        LOOP_BANKS = {"xnT": psA, "ctxT": psB, "gT": psC, "scores": psA, "probsT": psB, "uT": psC, "attn": psA,
                      "xfT": psB}
        own = [(psH[0], psH[1]), (psC, psD), (psA, psB), (psY[0], psY[1])]
        HEAD_BANKS = [{"xnT": i, "ctxT": j, "gT": j, "scores": i, "probsT": j, "uT": i, "attn": j, "xfT": i}
                      for i, j in own]
        LAST_BANKS = (psY[1], psA, psB, psC)
        ALL = range(TG)

        def n_is_last(g, e):
            return isinstance(g, int) and g * E + e == GROUPS * E - 1

        wq_in, small_in = sem("wq_in"), sem("small_in")
        x_in, ctx_in = [sem("x_in0"), sem("x_in_rest")], sem("ctx_in")
        w1_in = [sem(f"w1_in{p}") for p in range(PAIRS)]
        w2_in = [sem(f"w2_in{p}") for p in range(PAIRS)]
        out_done = sem("out_done")
        warm_zero = sem("warm_zero")
        const_zero, const_ready = sem("const_zero"), sem("const_ready")
        prep_ps, gram_ready, wqT_ready = sem("prep_ps"), sem("gram_ready"), sem("wqT_ready")
        b1_ready, small_hi, small_lo = sem("b1_ready"), sem("small_hi"), sem("small_lo")
        w1hi_ready, w1lo_ready = sem("w1hi_ready"), sem("w1lo_ready")
        w2hi_ready, w2lo_ready = sem("w2hi_ready"), sem("w2lo_ready")
        var_ready, rstd_ready, xn_ready = sem("var_ready"), sem("rstd_ready"), sem("xn_ready")
        xnT_ps, xnT_ready, ctxT_ps, ctxT_ready = sem("xnT_ps"), sem("xnT_ready"), sem("ctxT_ps"), sem("ctxT_ready")
        gT_ps, gT_ready, scores_ps, neg_ready = sem("gT_ps"), sem("gT_ready"), sem("scores_ps"), sem("neg_ready")
        probs_ready, probsT_ps, probsT_ready = sem("probs_ready"), sem("probsT_ps"), sem("probsT_ready")
        uT_ps, uT_ready, attn_ps = sem("uT_ps"), sem("uT_ready"), sem("attn_ps")
        x1_ready, var2_ready, rstd2_ready = sem("x1_ready"), sem("var2_ready"), sem("rstd2_ready")
        xf_ready, xfT_ps, xhi_ready, xlo_ready = sem("xf_ready"), sem("xfT_ps"), sem("xhi_ready"), sem("xlo_ready")
        base_ready = sem("base_ready")
        logits_ps, below_ready, gate_exp_ready = sem("logits_ps"), sem("below_ready"), sem("gate_exp_ready")
        cat_ready, catT_ps, catT_ready, b2_ps, b2_added = (
            sem("cat_ready"), sem("catT_ps"), sem("catT_ready"), sem("b2_ps"), sem("b2_added"))
        z_ps, h_ready, hlo0_ready, hlo_ready = sem("z_ps"), sem("h_ready"), sem("hlo0_ready"), sem("hlo_ready")
        y_ps, y_used = sem("y_ps"), sem("y_used")
        dve_chain, centred = sem("dve_chain"), sem("centred")

        block = stack.enter_context(nc.Block())

        def tiles(t):
            return t[:, :].rearrange("p (t n) -> p t n", n=P)

        XN_NEXT = 6
        CAT_T, B2_PRODUCT, B2_ADD = 3, 4, 5
        XN_T, GRAM, SCORES, MAX, EXPS, PROBS_T, CONTEXT, VALUES = 0, 1, 2, 2, 3, 5, 6, 7
        RESIDUAL, NORM2, XF_T, X_LO, LOGITS, GATE_TOP = 7, 8, 11, 11, 14, 14

        def head(stages, order=ALL):
            for wave in range(max(stages) + TG):
                for t in order:
                    if wave - t in stages:
                        stages[wave - t](t)

        def run(steps, slot):
            for at, step in steps:
                if at == slot:
                    step()

        def over(ap, n):
            return ap.unsqueeze(2).broadcast_to([P, TG, n])

        @block.sync
        def _(sp):
            sp.dma_start(x_sb[:, 0:TG, :], x_v[:, 0:TG, :]).then_inc(x_in[0], 16)
            sp.dma_start(ctx_sb[:, :, :], ctx_v[:, 0:TG, :]).then_inc(ctx_in, 16)

            def weights(p):
                e = slice(2 * p, 2 * p + 2)
                sp.dma_start(w1_sb[:, e, :], w1_v[:, e, :]).then_inc(w1_in[p], 16)
                sp.dma_start(w2_sb[:, e, :, :].rearrange("p e c n -> p (e c) n"),
                             w2_v[:, 2 * p * C:(2 * p + 2) * C, :]).then_inc(w2_in[p], 16)

            weights(0)
            sp.dma_start(x_sb[:, TG:, :], x_v[:, TG:, :]).then_inc(x_in[1], 16)
            sp.dma_start(gate_sb[:, :], gate_w).then_inc(small_in, 16)
            sp.dma_start(b1_rows[:, :], b1.rearrange("e (c p) -> (e c) p", p=P)).then_inc(small_in, 16)
            for q in range(3):
                sp.dma_start(b2_rows[32 * q:32 * q + E, :], b2).then_inc(small_in, 16)
            for p in range(1, PAIRS):
                weights(p)

            def next_context(a):
                sp.wait_ge(uT_ps, a * TG)
                sp.dma_start(ctx_sb[:, :, :], ctx_v[:, bass.ts(a, TG), :]).then_inc(ctx_in, 16)

            def store(g):
                sp.wait_ge(y_used, Y_FREE + (g + 1) * E)
                sp.dma_start(out_v[:, bass.ts(g, TG), :], acc[:, bass.ts(g, TG), :]).then_inc(out_done, 16)

            next_context(1)
            for g in range(0, GROUPS - 2):
                next_context(g + 2)
                store(g)
            store(GROUPS - 2)
            for t in range(0, TG, 2):
                i = (GROUPS - 1) * TG + t
                sp.wait_ge(y_used, Y_FREE + GROUPS * E - 1 + t + 2)
                sp.dma_start(out_v[:, i:i + 2, :], acc[:, i:i + 2, :]).then_inc(out_done, 16)
            sp.wait_ge(out_done, 16 * (GROUPS - 1 + TG // 2))

        @block.tensor
        def _(pe):
            def transposes(bank, src, ts, ready, wait=lambda t: None):
                for t in ts:
                    wait(t)
                    nc.tensor.transpose(tiles(bank)[:, t, :], src[:, t, :], ident[:, :]).then_inc(ready, 1)

            def xn_transposes(a, ts, banks):
                transposes(banks["xnT"], xn, ts, xnT_ps, lambda t: pe.wait_ge(xn_ready, a * TG + t + 1))

            def ctx_transposes(a, ts, banks):
                transposes(banks["ctxT"], ctx_sb, ts, ctxT_ps)

            def gram_product(a, ts, banks):
                pe.wait_ge(xnT_ready, a * TG + ts[-1] + 1)
                cols = slice(ts[0] * P, (ts[-1] + 1) * P)
                nc.tensor.matmul(banks["gT"][:, cols], gram[:, :], xnT[:, ts[0]:ts[-1] + 1, :], start=True,
                                 stop=True).then_inc(gT_ps, len(ts))

            def score_product(a, ts, banks):
                pe.wait_ge(gT_ready, a * TG + ts[-1] + 1)
                pe.wait_ge(ctxT_ready, a * TG + ts[-1] + 1)
                for t in ts:
                    nc.tensor.matmul(tiles(banks["scores"])[:, t, :], gT[:, t, :], ctxT[:, t, :], start=True,
                                     stop=True).then_inc(scores_ps, 1)

            def probs_transposes(a, ts, banks):
                transposes(banks["probsT"], probs, ts, probsT_ps, lambda t: pe.wait_ge(probs_ready, a * TG + t + 1))

            def context_product(a, ts, banks):
                pe.wait_ge(probsT_ready, a * TG + ts[-1] + 1)
                for t in ts:
                    nc.tensor.matmul(tiles(banks["uT"])[:, t, :], ctx_sb[:, t, :], probsT[:, t, :], start=True,
                                     stop=True).then_inc(uT_ps, 1)

            def value_product(a, ts, banks):
                pe.wait_ge(uT_ready, a * TG + ts[-1] + 1)
                for t in ts:
                    nc.tensor.matmul(tiles(banks["attn"])[:, t, :], uT[:, t, :], wqT[:, :], start=True,
                                     stop=True).then_inc(attn_ps, 1)

            def xf_transposes(a, ts, banks):
                transposes(banks["xfT"], xf, ts, xfT_ps, lambda t: pe.wait_ge(xf_ready, a * TG + t + 1))

            def logit_product(a):
                pe.wait_ge(xlo_ready, (a + 1) * TG)
                for t in range(TG):
                    o = psC[:, t * E:(t + 1) * E]
                    hi, lo = (v[:, a, t * P:(t + 1) * P] for v in (x_hi, x_lo))
                    nc.tensor.matmul(o, hi, gate_hi[:, :], start=True, stop=False)
                    nc.tensor.matmul(o, hi, gate_lo[:, :], start=False, stop=False)
                    last = nc.tensor.matmul(o, lo, gate_hi[:, :], start=False, stop=True)
                last.then_inc(logits_ps, 1)

            cat_ps = psD[0:NB2, 0:TG * P // 2].bitcast(fp16).rearrange("p (t n) -> p t n", n=P)

            def cat_transposes(g):
                pe.wait_ge(cat_ready, g + 1)
                for t in range(TG):
                    last = nc.tensor.transpose(cat_ps[:, t, :], weight_cat[:, t, :], ident16[:, :])
                last.then_inc(catT_ps, 1)

            def b2_product(g):
                pe.wait_ge(catT_ready, g + 1)
                for t in range(TG):
                    last = nc.tensor.matmul(tiles(psD)[:, t, :], weight_catT[:, t, :], b2_cat[:, :],
                                            start=True, stop=True)
                last.then_inc(b2_ps, 1)

            def hidden_product(g, e):
                u = (g * E + e) * C
                if e == 0:
                    pe.wait_ge(xhi_ready, (g + 1) * TG)
                pe.wait_ge(w1lo_ready, e // 2 + 1)
                for c in range(C):
                    pe.wait_ge(h_ready, u + c - 1)
                    w = slice(c * P, (c + 1) * P)
                    nc.tensor.matmul(psH[c][:, :], w1_hi[:, e, w], x_hi[:, g, :], start=True, stop=False)
                    nc.tensor.matmul(psH[c][:, :], w1_lo[:, e, w], x_hi[:, g, :], start=False, stop=False)
                    if e == 0 and c == 0:
                        pe.wait_ge(xlo_ready, (g + 1) * TG)
                    nc.tensor.matmul(psH[c][:, :], w1_hi[:, e, w], x_lo[:, g, :], start=False,
                                     stop=True).then_inc(z_ps, 1)

            def output_product(g, e):
                n = g * E + e
                i = e % 2
                split = is_split(g, e)
                if split:
                    pe.wait_ge(w2lo_ready, e // 2 + 1)
                else:
                    pe.wait_ge(w2_in[e // 2], 16)
                pe.wait_ge(h_ready, (n + 1) * C)
                pe.wait_ge(y_used, n + 1)
                last_expert = n_is_last(g, e)

                def add_product(t, hidden, weights, start, stop):
                    o = LAST_BANKS[t][:, 0:D] if last_expert else tiles(psY[i])[:, t, :]
                    for c in range(C):
                        last = nc.tensor.matmul(o, hidden[:, C * i + c, t * P:(t + 1) * P], weights[:, e, c, :],
                                                start=start and c == 0, stop=stop and c == C - 1)
                    if stop and (last_expert or t == TG - 1):
                        last.then_inc(y_ps, 1)

                for t in range(TG):
                    if split:
                        add_product(t, h_hi, w2_hi, last_expert or t == 0, False)
                        add_product(t, h_hi, w2_lo, False, False)
                    else:
                        add_product(t, h, w2_sb, True, True)
                if split:
                    pe.wait_ge(hlo_ready, splits(g, e))
                    pe.wait_ge(hlo0_ready, splits(g, e))
                    for t in range(TG):
                        add_product(t, h_lo, w2_hi, False, last_expert or t == TG - 1)

            def group(g, attention):
                a, banks = g + 1, LOOP_BANKS

                def ctx_step():
                    pe.wait_ge(ctx_in, 16 * (a + 1))
                    ctx_transposes(a, ALL, banks)

                def gram_step():
                    pe.wait_ge(below_ready, a)
                    gram_product(a, ALL, banks)

                steps = [(CAT_T, lambda: cat_transposes(g)), (B2_PRODUCT, lambda: b2_product(g))]
                if attention:
                    steps += [(XN_T, lambda: xn_transposes(a, ALL, banks)), (XN_T, ctx_step),
                              (GRAM, gram_step),
                              (SCORES, lambda: score_product(a, ALL, banks)),
                              (PROBS_T, lambda: probs_transposes(a, ALL, banks)),
                              (CONTEXT, lambda: context_product(a, ALL, banks)), (VALUES, lambda: value_product(a, ALL, banks)),
                              (XF_T, lambda: xf_transposes(a, ALL, banks)), (LOGITS, lambda: logit_product(a))]
                for e in range(E):
                    if e < E - 1:
                        hidden_product(g, e + 1)
                    elif attention:
                        hidden_product(g + 1, 0)
                    run(steps, 2 * e)
                    output_product(g, e)
                    run(steps, 2 * e + 1)

            pe.wait_ge(warm_zero, 1)
            for _ in range(WARM_UP):
                nc.tensor.matmul(psA[:, :], warm[:, 0:P], warm[:, :], start=True, stop=True)

            pe.wait_ge(const_ready, 1)
            pe.wait_ge(wq_in, 16)
            nc.tensor.matmul(psY[1][:, 0:D], wq_sb[:, :], wq_sb[:, :], start=True, stop=True)
            nc.tensor.transpose(psY[1][:, D:2 * D], wq_sb[:, :], ident[:, :]).then_inc(prep_ps, 1)

            def both_transposes(t):
                banks = HEAD_BANKS[t]
                if t == 0:
                    pe.wait_ge(ctx_in, 16)
                ctx_transposes(0, [t], banks)
                xn_transposes(0, [t], banks)

            def first_gram(t):
                if t == 0:
                    pe.wait_ge(wqT_ready, 1)
                gram_product(0, [t], HEAD_BANKS[t])

            def stage(product):
                return lambda t: product(0, [t], HEAD_BANKS[t])

            head({0: both_transposes, 1: first_gram, 2: stage(score_product), 3: stage(probs_transposes),
                  4: stage(context_product), 5: stage(value_product), 9: stage(xf_transposes)})
            pe.wait_ge(x1_ready, 2)
            pe.wait_ge(small_in, 16 * 5)
            nc.tensor.transpose(psD[:, 0:E * C], b1_rows[:, :], ident[0:E * C, 0:E * C]).then_inc(prep_ps, 1)
            pe.wait_ge(w1lo_ready, 1)
            for t in range(TG):
                pe.wait_ge(xlo_ready, t + 1)
                tok = slice(t * P, (t + 1) * P)
                for c in range(C):
                    w = slice(c * P, (c + 1) * P)
                    nc.tensor.matmul(psH[c][:, tok], w1_hi[:, 0, w], x_hi[:, 0, tok], start=True, stop=False)
                    nc.tensor.matmul(psH[c][:, tok], w1_hi[:, 0, w], x_lo[:, 0, tok], start=False, stop=False)
                    last = nc.tensor.matmul(psH[c][:, tok], w1_lo[:, 0, w], x_hi[:, 0, tok], start=False, stop=True)
                    if t == TG - 1:
                        last.then_inc(z_ps, 1)
            pe.wait_ge(small_lo, 1)
            logit_product(0)
            for g in range(0, GROUPS - 1):
                group(g, True)
            group(GROUPS - 1, False)

        @block.scalar
        def _(act):
            def copy(dst, src, ready, scale=1.0):
                nc.scalar.activation(dst, src, ACT.Copy, scale=scale).then_inc(ready, 1)

            def evacuate(dst, bank, ps, ready, scale=1.0):
                def step(a, ts, banks):
                    act.wait_ge(ps, a * TG + ts[-1] + 1)
                    v = slice(ts[0], ts[-1] + 1)
                    nc.scalar.activation(dst[:, v, :], tiles(banks[bank])[:, v, :], ACT.Copy,
                                         scale=scale).then_inc(ready, len(ts))
                return step

            xn_out = evacuate(xnT, "xnT", xnT_ps, xnT_ready)
            ctx_out = evacuate(ctxT, "ctxT", ctxT_ps, ctxT_ready)
            gram_out = evacuate(gT, "gT", gT_ps, gT_ready)
            probs_out = evacuate(probsT, "probsT", probsT_ps, probsT_ready)
            context_out = evacuate(uT, "uT", uT_ps, uT_ready)

            def softmax(a, ts, banks):
                for t in ts:
                    act.wait_ge(neg_ready, a * TG + t + 1)
                    nc.scalar.activation(probs[:, t, :], neg_s[:, t, :], ACT.Exp, bias=neg_max[:, t:t + 1],
                                         scale=-1.0, accum_out=row_sum[:, t:t + 1]).then_inc(probs_ready, 1)

            def x_hi_part(a, ts, banks):
                act.wait_ge(xfT_ps, a * TG + ts[-1] + 1)
                cols = slice(ts[0] * P, (ts[-1] + 1) * P)
                nc.scalar.activation(x_hi[:, a, cols], banks["xfT"][:, cols], ACT.Copy,
                                     scale=SX).then_inc(xhi_ready, len(ts))

            def gate_exps(a):
                act.wait_ge(below_ready, a + 1)
                nc.scalar.activation(gate_exp[:, :, :], below[:, :, :], ACT.Exp).then_inc(gate_exp_ready, 1)

            cat_ps = psD[0:NB2, 0:TG * P // 2].bitcast(fp16).rearrange("p (t n) -> p t n", n=P)

            def cat_out(g):
                act.wait_ge(catT_ps, g + 1)
                copy(weight_catT[:, :, :], cat_ps, catT_ready)

            def hidden_relu(g, e):
                n = g * E + e
                for c in range(C):
                    act.wait_ge(z_ps, n * C + c + 1)
                    scale = SH / (SX * SW) if is_split(g, e) else 1.0
                    bias = b1T[:, int(is_split(g, e)), e * C + c:e * C + c + 1]
                    if is_split(g, e):
                        nc.scalar.activation(h_hi[:, C * (e % 2) + c, :], psH[c][:, :], ACT.Relu, bias=bias, scale=scale)
                    nc.scalar.activation(h[:, C * (e % 2) + c, :], psH[c][:, :], ACT.Relu, bias=bias,
                                         scale=scale).then_inc(h_ready, 1)

            def group(g, attention):
                a = g + 1
                steps = [(CAT_T, lambda: cat_out(g))]
                banks = LOOP_BANKS
                if attention:
                    steps += [(XN_T, lambda: xn_out(a, ALL, banks)), (XN_T, lambda: ctx_out(a, ALL, banks)),
                              (GRAM, lambda: gram_out(a, ALL, banks)), (EXPS, lambda: softmax(a, ALL, banks)),
                              (PROBS_T, lambda: probs_out(a, ALL, banks)),
                              (CONTEXT, lambda: context_out(a, ALL, banks)),
                              (XF_T, lambda: x_hi_part(a, ALL, banks)), (GATE_TOP, lambda: gate_exps(a))]
                for e in range(E):
                    if e < E - 1:
                        hidden_relu(g, e + 1)
                    elif attention:
                        hidden_relu(g + 1, 0)
                    run(steps, 2 * e)
                    run(steps, 2 * e + 1)

            act.dma_start(wq_sb[:, :], wq).then_inc(wq_in, 16)

            def w1_hi_part(p):
                act.wait_ge(w1_in[p], 16)
                copy(w1_hi[:, 2 * p:2 * p + 2, :], w1_sb[:, 2 * p:2 * p + 2, :], w1hi_ready, scale=SW)

            def w2_hi_part(p):
                act.wait_ge(w2_in[p], 16)
                copy(w2_hi[:, 2 * p:2 * p + 2, :, :], w2_sb[:, 2 * p:2 * p + 2, :, :], w2hi_ready, scale=SW)

            act.wait_ge(prep_ps, 1)
            copy(gram[:, :], psY[1][:, 0:D], gram_ready, scale=-SCALE)
            copy(wqT[:, :], psY[1][:, D:2 * D], wqT_ready)

            def both_out(t):
                ctx_out(0, [t], HEAD_BANKS[t])
                xn_out(0, [t], HEAD_BANKS[t])

            def stage(step):
                return lambda t: step(0, [t], HEAD_BANKS[t])

            def second_weights(t):
                if t == 0:
                    w1_hi_part(1)
                    w2_hi_part(1)

            head({0: both_out, 1: stage(gram_out), 2: stage(softmax), 3: stage(probs_out),
                  4: stage(context_out), 8: second_weights, 9: stage(x_hi_part)})
            act.wait_ge(prep_ps, 2)
            nc.scalar.activation(b1T[:, 0, :], psD[:, 0:E * C], ACT.Copy, scale=SX * SW)
            copy(b1T[:, 1, :], psD[:, 0:E * C], b1_ready, scale=SH)
            act.wait_ge(b1_ready, 1)
            w1_hi_part(2)
            w2_hi_part(2)
            hidden_relu(0, 0)
            gate_exps(0)
            w1_hi_part(3)
            w2_hi_part(3)
            for g in range(0, GROUPS - 1):
                group(g, True)
            group(GROUPS - 1, False)

        @block.gpsimd
        def _(pool):
            nc.gpsimd.memset(ident[:, :], 0.0).then_inc(const_zero, 1)
            nc.gpsimd.memset(ident16[:, :], 0.0).then_inc(const_zero, 1)
            nc.gpsimd.memset(mask[:, :], 0.0).then_inc(const_zero, 1)
            pool.wait_ge(const_zero, 3)
            nc.gpsimd.affine_select(out=ident[:, :], in_=ident[:, :], compare_op=ALU.not_equal, fill=1.0, base=0,
                                    pattern=[[-1, P]], channel_multiplier=1).then_inc(const_ready, 1)
            nc.gpsimd.affine_select(out=ident16[:, :], in_=ident16[:, :], compare_op=ALU.not_equal, fill=1.0,
                                    base=0, pattern=[[-1, P]], channel_multiplier=1).then_inc(const_zero, 1)
            nc.gpsimd.affine_select(out=mask[:, :], in_=mask[:, :], compare_op=ALU.is_ge, fill=MASKED, base=0,
                                    pattern=[[-1, P]], channel_multiplier=1).then_inc(const_zero, 1)
            pool.wait_ge(const_zero, 5)
            nc.gpsimd.memset(mask[SEQ:P, 0:SEQ], MASKED).then_inc(const_zero, 1)
            pool.wait_ge(const_zero, 6)
            nc.gpsimd.memset(restart[:, :, :], 1.0).then_inc(const_zero, 1)
            pool.wait_ge(const_zero, 7)
            nc.gpsimd.memset(restart[:, :, 0:1], 0.0)
            nc.gpsimd.memset(half[:, :], -0.5).then_inc(const_ready, 1)
            nc.gpsimd.memset(weight_cat[:, :, :], 0.0).then_inc(const_ready, 1)
            nc.gpsimd.memset(b2_cat[:, :], 0.0).then_inc(const_ready, 1)
            pool.wait_ge(const_ready, 4)

            def attention_rstd(a, ts):
                v = slice(ts[0], ts[-1] + 1)
                pool.wait_ge(var2_ready, a * TG + ts[-1] + 1)
                nc.gpsimd.tensor_tensor(rstd2[:, v], var2[:, v], half[:, v], ALU.pow).then_inc(rstd2_ready, len(ts))

            def first_rstd(t, n):
                nc.gpsimd.tensor_tensor(rstd[:, bass.ds(t, n)], mv[:, bass.ds(t, n), 1], half[:, 0:n],
                                        ALU.pow).then_inc(rstd_ready, n)

            def first_norm(a):
                pool.wait_ge(xnT_ps, a * TG)
                mean, inv = (over(v, D) for v in (mv[:, bass.ts(a, TG), 0], rstd[:, bass.ts(a, TG)]))
                first_rstd(a * TG, TG)
                nc.gpsimd.tensor_tensor(xn[:, :, :], x_sb[:, bass.ts(a, TG), :], mean, ALU.subtract).then_inc(centred, 1)
                pool.wait_ge(centred, a)
                pool.wait_ge(rstd_ready, (a + 1) * TG)
                nc.gpsimd.tensor_tensor(xn[:, :, :], xn[:, :, :], inv, ALU.mult).then_inc(xn_ready, TG)

            def base_sum(a):
                pool.wait_ge(xf_ready, (a + 1) * TG)
                nc.gpsimd.tensor_tensor(acc[:, bass.ts(a, TG), :], x1[:, :, :], xf[:, :, :],
                                        ALU.add).then_inc(base_ready, 1)

            def hidden_lo0(g, e):
                if is_split(g, e):
                    i = C * (e % 2)
                    pool.wait_ge(h_ready, (g * E + e) * C + 1)
                    nc.gpsimd.tensor_tensor(h_lo[:, i, :], h[:, i, :], h_hi[:, i, :],
                                            ALU.subtract).then_inc(hlo0_ready, 1)

            def group(g, attention, norm):
                a = g + 1
                steps = [(NORM2, lambda: attention_rstd(a, ALL)), (XF_T, lambda: base_sum(a))] if attention else []
                if norm:
                    steps += [(XN_NEXT, lambda: first_norm(a + 1))]
                for e in range(E):
                    if e < E - 1:
                        hidden_lo0(g, e + 1)
                    elif attention:
                        hidden_lo0(g + 1, 0)
                    run(steps, 2 * e)
                    run(steps, 2 * e + 1)

            for t in range(TG):
                pool.wait_ge(var_ready, t + 1)
                first_rstd(t, 1)
            pool.wait_ge(w1_in[0], 16)
            nc.gpsimd.tensor_scalar(w1_hi[:, 0:2, :], w1_sb[:, 0:2, :], SW, None, ALU.mult).then_inc(w1hi_ready, 1)
            pool.wait_ge(w2_in[0], 16)
            nc.gpsimd.tensor_scalar(w2_hi[:, 0:2, :, :], w2_sb[:, 0:2, :, :], SW, None,
                                    ALU.mult).then_inc(w2hi_ready, 1)
            pool.wait_ge(var_ready, 2 * TG)
            first_norm(1)
            for t in range(TG):
                attention_rstd(0, [t])
            base_sum(0)
            hidden_lo0(0, 0)
            pool.wait_ge(var_ready, TILES)
            for g in range(0, GROUPS - 2):
                group(g, True, True)
            group(GROUPS - 2, True, False)
            group(GROUPS - 1, False, False)

        @block.vector
        def _(dve):
            def row_stats(t):
                return nc.vector.bn_stats(stats[:, t, :], x_sb[:, t, :])

            def mean_and_var(t0, t1, chain):
                for t in range(t0, t1):
                    last = nc.vector.bn_aggr(mv[:, t, :], stats[:, t, :])
                chain.link(last)
                nc.vector.tensor_scalar(mv[:, t0:t1, 1], mv[:, t0:t1, 1], EPS, None, ALU.add).then_inc(var_ready, t1 - t0)

            def first_norm(t):
                dve.wait_ge(rstd_ready, t + 1)
                nc.vector.tensor_scalar(xn[:, t, :], x_sb[:, t, :], mv[:, t, 0:1], rstd[:, t:t + 1],
                                        ALU.subtract, ALU.mult).then_inc(xn_ready, 1)

            def mask_and_max(a, ts, banks):
                dve.wait_ge(scores_ps, a * TG + ts[-1] + 1)
                for t in ts:
                    nc.vector.tensor_tensor_reduce(
                        out=neg_s[:, t, :], in0=tiles(banks["scores"])[:, t, :], in1=mask[:, :], scale=1.0,
                        scalar=3e38, op0=ALU.add, op1=ALU.min,
                        accum_out=neg_max[:, t:t + 1]).then_inc(neg_ready, 1)

            def invert_sums(a, ts, chain):
                v = slice(ts[0], ts[-1] + 1)
                dve.wait_ge(probs_ready, a * TG + ts[-1] + 1)
                chain.mark(nc.vector.reciprocal(inv_sum[:, v], row_sum[:, v]))

            def residual_and_norm(a, ts, banks, chain):
                v = slice(ts[0], ts[-1] + 1)
                chain.wait()
                dve.wait_ge(attn_ps, a * TG + ts[-1] + 1)
                for t in ts:
                    last = nc.vector.scalar_tensor_tensor(
                        out=x1[:, t, :], in0=tiles(banks["attn"])[:, t, :], scalar=inv_sum[:, t:t + 1],
                        in1=x_sb[:, a * TG + t, :], op0=ALU.mult, op1=ALU.add)
                last.then_inc(x1_ready, len(ts))
                dve.wait_ge(x1_ready, a * TG + ts[-1] + 1)
                for t in ts:
                    last = nc.vector.bn_stats(stats2[:, t, :], x1[:, t, :])
                chain.link(last)
                for t in ts:
                    last = nc.vector.bn_aggr(mv2[:, t, :], stats2[:, t, :])
                chain.link(last)
                nc.vector.tensor_scalar(var2[:, v], mv2[:, v, 1], EPS, None, ALU.add).then_inc(var2_ready, len(ts))

            def second_norm(a, ts):
                for t in ts:
                    dve.wait_ge(rstd2_ready, a * TG + t + 1)
                    nc.vector.tensor_scalar(xf[:, t, :], x1[:, t, :], mv2[:, t, 0:1], rstd2[:, t:t + 1],
                                            ALU.subtract, ALU.mult).then_inc(xf_ready, 1)

            def x_lo_part(a, ts, banks):
                dve.wait_ge(xhi_ready, a * TG + ts[-1] + 1)
                cols = slice(ts[0] * P, (ts[-1] + 1) * P)
                nc.vector.scalar_tensor_tensor(out=x_lo[:, a, cols], in0=banks["xfT"][:, cols], scalar=SX,
                                               in1=x_hi[:, a, cols], op0=ALU.mult,
                                               op1=ALU.subtract).then_inc(xlo_ready, len(ts))

            first, second = top8[:, :, 0], top8[:, :, 1]
            TT = nc.vector.tensor_tensor

            def gate_top(a, chain):
                dve.wait_ge(logits_ps, a + 1)
                chain.link(nc.vector.tensor_scalar(logits[:, :, :], psC[:, 0:TG * E].rearrange("p (t e) -> p t e", e=E),
                                                   1.0 / (SX * SW), None, ALU.mult))
                for t in range(TG):
                    last = nc.vector.max(top8[:, t, :], logits[:, t, :])
                chain.link(last)
                TT(below[:, :, :], logits[:, :, :], over(first, E), ALU.subtract).then_inc(below_ready, 1)
                TT(is_second[:, :, :], logits[:, :, :], over(second, E), ALU.is_equal)
                TT(one_above[:, :], first, second, ALU.is_gt)
                chain.link(TT(above[:, :, :], logits[:, :, :], over(second, E), ALU.is_gt))

            def gate_choice(a, chain, meanwhile):
                between = meanwhile or [None] * 4
                chain.link(nc.vector.tensor_tensor_scan(
                    nth[:, :, :].rearrange("p t e -> p (t e)"), restart[:, :, :].rearrange("p t e -> p (t e)"),
                    is_second[:, :, :].rearrange("p t e -> p (t e)"), 0.0, ALU.mult, ALU.add), between[0])
                chain.link(TT(nth[:, :, :], nth[:, :, :], over(one_above[:, :], E), ALU.add), between[1])
                chain.link(nc.vector.scalar_tensor_tensor(out=chosen[:, :, :], in0=nth[:, :, :], scalar=2.0,
                                                          in1=is_second[:, :, :], op0=ALU.is_le, op1=ALU.mult),
                           between[2])
                chain.link(TT(chosen[:, :, :], chosen[:, :, :], above[:, :, :], ALU.add), between[3])

            def gate_weights(a, chain):
                dve.wait_ge(gate_exp_ready, a + 1)
                chain.link(TT(chosen[:, :, :], chosen[:, :, :], gate_exp[:, :, :], ALU.mult))
                nc.vector.reduce_sum(sum_two[:, :], chosen[:, :, :], axis=AX.X)
                chain.link(nc.vector.reduce_sum(sum_all[:, :], gate_exp[:, :, :], axis=AX.X))
                chain.link(nc.vector.scalar_tensor_tensor(out=sum_two[:, :], in0=sum_all[:, :], scalar=1e-8,
                                                          in1=sum_two[:, :], op0=ALU.mult, op1=ALU.add))
                chain.link(nc.vector.reciprocal(inv_two[:, :], sum_two[:, :]))
                chain.link(TT(weight[:, :, :], chosen[:, :, :], over(inv_two[:, :], E), ALU.mult))
                dve.wait_ge(y_used, Y_FREE + a * E)
                nc.vector.tensor_scalar(weight_y[:, :, :], weight[:, :, :], 1.0 / (SH * SW), None, ALU.mult)
                nc.vector.tensor_scalar(weight_cat[:, :, 64:64 + E], weight[:, :, :], SX, None, ALU.mult)
                chain.link(nc.vector.tensor_scalar(weight_cat[:, :, 0:E], weight[:, :, :], SX, None, ALU.mult))
                nc.vector.scalar_tensor_tensor(out=weight_cat[:, :, 32:32 + E], in0=weight[:, :, :], scalar=SX,
                                               in1=weight_cat[:, :, 0:E], op0=ALU.mult,
                                               op1=ALU.subtract).then_inc(cat_ready, 1)
                dve.wait_ge(cat_ready, a + 1)

            def hidden_lo(g, e):
                if is_split(g, e):
                    i = C * (e % 2) + 1
                    dve.wait_ge(h_ready, (g * E + e + 1) * C)
                    nc.vector.tensor_tensor(h_lo[:, i, :], h[:, i, :], h_hi[:, i, :],
                                            ALU.subtract).then_inc(hlo_ready, 1)

            def add_expert(g, e):
                n = g * E + e
                dve.wait_ge(y_ps, n + 1)
                if e == 0:
                    dve.wait_ge(base_ready, g + 1)
                else:
                    dve.wait_ge(y_used, Y_FREE + n)
                for t in range(TG):
                    o = acc[:, g * TG + t, :]
                    y = tiles(psY[e % 2])[:, t, :]
                    if n_is_last(g, e):
                        dve.wait_ge(y_ps, n + t + 1)
                        y = LAST_BANKS[t][:, 0:D]
                    last = nc.vector.scalar_tensor_tensor(out=o, in0=y, scalar=weight_y[:, t, e:e + 1], in1=o,
                                                          op0=ALU.mult, op1=ALU.add)
                    if n_is_last(g, e):
                        last.then_inc(y_used, 1)
                if not n_is_last(g, e):
                    last.then_inc(y_used, 1)

            def add_b2(g):
                dve.wait_ge(b2_ps, g + 1)
                dve.wait_ge(y_used, Y_FREE + g * E + 3)
                o = acc[:, bass.ts(g, TG), :]
                nc.vector.scalar_tensor_tensor(out=o, in0=tiles(psD), scalar=1.0 / (SX * SW), in1=o,
                                               op0=ALU.mult, op1=ALU.add).then_inc(b2_added, 1)
                dve.wait_ge(b2_added, g + 1)

            LINKS = 2 + 14

            def group(g, attention, chain):
                a = g + 1
                steps = [(B2_ADD, lambda: add_b2(g))]
                if attention:
                    banks = LOOP_BANKS
                    steps += [(MAX, lambda: mask_and_max(a, ALL, banks)),
                              (RESIDUAL, lambda: invert_sums(a, ALL, chain)), (RESIDUAL, lambda: residual_and_norm(a, ALL, banks, chain)),
                              (NORM2, lambda: second_norm(a, ALL)), (X_LO, lambda: x_lo_part(a, ALL, banks)),
                              (GATE_TOP, lambda: gate_top(a, chain))]
                gate_choice(g, chain, [lambda: hidden_lo(g, 1), None, None, None])
                gate_weights(g, chain)
                for e in range(E):
                    if 0 < e < E - 1:
                        hidden_lo(g, e + 1)
                    elif e and attention:
                        hidden_lo(g + 1, 0)
                    run(steps, 2 * e)
                    add_expert(g, e)
                    run(steps, 2 * e + 1)

            nc.vector.memset(warm[:, :], 0.0).then_inc(warm_zero, 1)
            dve.sem_inc(y_used, Y_FREE)
            chain = Chain(dve, dve_chain)
            dve.wait_ge(x_in[0], 16)
            for t in range(TG):
                chain.link(row_stats(t))
                mean_and_var(t, t + 1, chain)
            for t in range(TG):
                first_norm(t)

            def first_residual(t):
                residual_and_norm(0, [t], HEAD_BANKS[t], chain)

            def w1_lo_part(p):
                dve.wait_ge(w1hi_ready, p + 1)
                w = (slice(None), slice(2 * p, 2 * p + 2), slice(None))
                nc.vector.scalar_tensor_tensor(out=w1_lo[w], in0=w1_sb[w], scalar=SW, in1=w1_hi[w],
                                               op0=ALU.mult, op1=ALU.subtract).then_inc(w1lo_ready, 1)

            def w2_lo_part(p):
                dve.wait_ge(w2hi_ready, p + 1)
                w = (slice(None), slice(2 * p, 2 * p + 2), slice(None), slice(None))
                nc.vector.scalar_tensor_tensor(out=w2_lo[w], in0=w2_sb[w], scalar=SW, in1=w2_hi[w],
                                               op0=ALU.mult, op1=ALU.subtract).then_inc(w2lo_ready, 1)

            def small_parts():
                dve.wait_ge(small_in, 16 * 5)
                dve.wait_ge(const_ready, 4)
                nc.vector.tensor_scalar(gate_hi[:, :], gate_sb[:, :], SW, None, ALU.mult)
                rows = [slice(32 * q, 32 * q + E) for q in range(3)]
                for r in rows:
                    last = nc.vector.tensor_scalar(b2_cat[r, :], b2_rows[r, :], SW, None, ALU.mult)
                last.then_inc(small_hi, 1)
                dve.wait_ge(small_hi, 1)
                nc.vector.scalar_tensor_tensor(out=gate_lo[:, :], in0=gate_sb[:, :], scalar=SW, in1=gate_hi[:, :],
                                               op0=ALU.mult, op1=ALU.subtract)
                nc.vector.scalar_tensor_tensor(out=b2_cat[rows[2], :], in0=b2_rows[rows[2], :], scalar=SW,
                                               in1=b2_cat[rows[2], :], op0=ALU.mult,
                                               op1=ALU.subtract).then_inc(small_lo, 1)

            def second_group_stats():
                dve.wait_ge(x_in[1], 16)
                for t in range(TG, 2 * TG):
                    last = row_stats(t)
                chain.link(last)
                mean_and_var(TG, 2 * TG, chain)

            def more_stats(n):
                for t in range((n + 1) * TG, (n + 2) * TG):
                    last = row_stats(t)
                return last

            def first_max(t):
                mask_and_max(0, [t], HEAD_BANKS[t])
                for part in ([small_parts], [second_group_stats],
                             [lambda: more_stats(1), lambda: w1_lo_part(0)], [])[t]:
                    part()

            head({2: first_max, 4: lambda t: invert_sums(0, [t], chain), 5: first_residual,
                  7: lambda t: second_norm(0, [t]), 10: lambda t: x_lo_part(0, [t], HEAD_BANKS[t])}, order=ALL[::-1])
            chain.mark(more_stats(2))
            w2_lo_part(0)
            w1_lo_part(1)
            w2_lo_part(1)
            chain.wait()
            mean_and_var(2 * TG, TILES, chain)
            hidden_lo(0, 0)
            gate_top(0, chain)
            for p in range(2, PAIRS):
                w1_lo_part(p)
                w2_lo_part(p)
            LINKS_BEFORE = chain.count
            for g in range(0, GROUPS - 1):
                inner = Chain(dve, dve_chain, LINKS_BEFORE + g * LINKS)
                group(g, True, inner)
                assert inner.count == LINKS, inner.count
            group(GROUPS - 1, False, Chain(dve, dve_chain, LINKS_BEFORE + (GROUPS - 1) * LINKS))


_INS = ['x', 'ctx_1024', 'L0_xattn_Wq', 'L0_ffn_gate_W', 'L0_ffn_W1', 'L0_ffn_b1', 'L0_ffn_W2', 'L0_ffn_b2']
_OUTS = [((32, 64, 128), 'float32')]


def kernel(**inputs):
    import numpy as _np
    import concourse.bacc as _bacc
    from concourse import mybir as _mybir
    from concourse.bass_utils import run_bass_kernel_spmd as _run

    nc = _bacc.Bacc("TRN2", target_bir_lowering=False, num_devices=1)
    arrays, args = {}, []
    for name in _INS:
        a = _np.ascontiguousarray(inputs[name])
        arrays[f"in_{name}_dram"] = a
        args.append(nc.dram_tensor(f"in_{name}_dram", a.shape, _mybir.dt.from_np(a.dtype), kind="ExternalInput").ap())
    for i, (shape, dtype) in enumerate(_OUTS):
        dt = _mybir.dt.from_np(_np.dtype(dtype))
        args.append(nc.dram_tensor(f"out_{i}_dram", shape, dt, kind="ExternalOutput").ap())
    xattn_moe(nc, *args)
    r = _run(nc, [arrays], core_ids=[0])
    return r.results[0]["out_0_dram"]
```
